# Optimizing a Trainium2 kernel written in Bass

```python
import numpy as np
import jax
import jax.numpy as jnp

def _softmax(x, axis=-1):
    return jax.nn.softmax(x, axis=axis)

def _gelu(x):
    return jax.nn.gelu(x, approximate=True)

def _silu(x):
    return jax.nn.silu(x)

def _sigmoid(x):
    return jax.nn.sigmoid(x)

def _layernorm(x, axis=-1, eps=1e-05):
    m = jnp.mean(x, axis=axis, keepdims=True)
    v = jnp.var(x, axis=axis, keepdims=True)
    return (x - m) / jnp.sqrt(v + eps)

def _scatter_add(tgt, idx, src, axis=0):
    return tgt.at[idx].add(src)

def _segment_sum(src, seg, n):
    return jax.ops.segment_sum(src, seg, n)
kernel_name = 'mk_vit_tower_d1_tok_img4096_r4_60071d'

def setup_inputs(seed: int=0):
    np.random.seed(seed)
    _w = jnp.asarray

    def _rec_inputs():
        import jax
        import jax.numpy as jnp
        _rk = jax.random.key(seed)
        x = -0.00348982 + 0.707501 * jax.random.normal(jax.random.fold_in(_rk, 1), (16, 128, 64, 2), jnp.float32)
        return x
    x = _rec_inputs()

    def _L0_tok_setup():
        import jax, jax.numpy as jnp
        import numpy as np
        H, N, S, CH, LEN = (128, 64, 128, 1, 1024)

        def _s4d_kernel(log_dt, C, B, inv_A_real, A_imag, L):
            dt = jnp.exp(log_dt)
            Cc = C[..., 0] + 1j * C[..., 1]
            Bc = B[..., 0] + 1j * B[..., 1]
            A = -jnp.exp(inv_A_real) + 1j * A_imag
            rep = H // A.shape[0]
            A = jnp.tile(A, (rep, 1))
            Bc = jnp.tile(Bc, (rep, 1))
            dtA = A * dt[:, None]
            Cc = Bc[None, :, :] * Cc
            Cc = Cc * (jnp.exp(dtA) - 1.0) / A
            ell = jnp.arange(L, dtype=jnp.float32)
            V = jnp.exp(dtA[:, :, None] * ell)
            K = 2.0 * jnp.einsum('chn,hnl->chl', Cc, V).real
            return K.astype(jnp.float32)
        key = jax.random.key(seed)
        k1, k2 = jax.random.split(key, 2)
        log_dt = jax.random.uniform(k1, (H,), minval=float(np.log(0.001)), maxval=float(np.log(0.1))).astype(jnp.float32)
        inv_A_real = jnp.full((S, N), float(np.log(0.5)), dtype=jnp.float32)
        A_imag = jnp.tile((np.pi * jnp.arange(N, dtype=jnp.float32))[None, :], (S, 1))
        B = jnp.stack([jnp.ones((S, N), jnp.float32), jnp.zeros((S, N), jnp.float32)], axis=-1)
        C = (jax.random.normal(k2, (CH, H, N, 2)) * 0.5 ** 0.5).astype(jnp.float32)
        return {'log_dt': log_dt, 'C': C, 'B': B, 'inv_A_real': inv_A_real, 'A_imag': A_imag, 'L': LEN}
    _L0_tok_all = _L0_tok_setup()
    _L0_tok_in = {k: v for k, v in _L0_tok_all.items() if k in ('log_dt', 'B', 'inv_A_real', 'A_imag')}
    del _L0_tok_all

    def _L0_attn_setup():
        import jax, jax.numpy as jnp
        import numpy as np
        import math
        B, S, D = (1, 512, 1024)
        H, KV, HD = (32, 8, 128)
        GROUPS = H // KV
        SYS_LEN, IMG_LEN = (35, 144)
        ENH, SUP = (1.5, 0.5)
        ROPE_BASE = 10000.0

        def _rope_cos_sin(seq_len, dtype):
            inv_freq = 1.0 / ROPE_BASE ** (jnp.arange(0, HD, 2, dtype=jnp.float32) / HD)
            pos = jnp.arange(seq_len, dtype=jnp.float32)
            freqs = pos[:, None] * inv_freq[None, :]
            emb = jnp.concatenate([freqs, freqs], axis=-1)
            return (jnp.cos(emb).astype(dtype), jnp.sin(emb).astype(dtype))

        def _rotate_half(x):
            x1, x2 = (x[..., :HD // 2], x[..., HD // 2:])
            return jnp.concatenate([-x2, x1], axis=-1)
        key = jax.random.key(seed)
        ks = jax.random.split(key, 5)
        scale = 0.02
        return {'hidden_states': jax.random.normal(ks[0], (B, S, D), dtype=jnp.float32), 'wq': jax.random.normal(ks[1], (H * HD, D), dtype=jnp.float32) * scale, 'wk': jax.random.normal(ks[2], (KV * HD, D), dtype=jnp.float32) * scale, 'wv': jax.random.normal(ks[3], (KV * HD, D), dtype=jnp.float32) * scale, 'wo': jax.random.normal(ks[4], (D, H * HD), dtype=jnp.float32) * scale}
    _L0_attn_all = _L0_attn_setup()
    _L0_attn_in = {k: v for k, v in _L0_attn_all.items() if k in ('wq', 'wk', 'wv', 'wo')}
    del _L0_attn_all

    def _L0_ffn_setup():
        import jax, jax.numpy as jnp
        import numpy as np
        key = jax.random.key(seed)
        k = jax.random.split(key, 6)
        x = jax.random.normal(k[0], (4, 512, 1024), jnp.float32)
        W = jax.random.normal(k[1], (1024, 1024), jnp.float32) * 0.02
        bias = jax.random.normal(k[2], (1024,), jnp.float32) * 0.02
        A = jax.random.normal(k[3], (16, 16, 1024), jnp.float32) * 0.02
        Bf = jax.random.normal(k[4], (16, 1024, 16), jnp.float32) * 0.02
        coeffs = jax.random.uniform(k[5], (16,), jnp.float32)
        scales = jnp.full((16,), 0.5, jnp.float32)
        return {'x': x, 'W': W, 'bias': bias, 'A': A, 'Bf': Bf, 'coeffs': coeffs, 'scales': scales}
    _L0_ffn_all = _L0_ffn_setup()
    _L0_ffn_in = {k: v for k, v in _L0_ffn_all.items() if k in ('W', 'bias', 'A', 'Bf', 'coeffs', 'scales')}
    del _L0_ffn_all
    return {'x': x, 'L0_tok_log_dt': _L0_tok_in['log_dt'], 'L0_tok_B': _L0_tok_in['B'], 'L0_tok_inv_A_real': _L0_tok_in['inv_A_real'], 'L0_tok_A_imag': _L0_tok_in['A_imag'], 'L0_attn_wq': _L0_attn_in['wq'], 'L0_attn_wk': _L0_attn_in['wk'], 'L0_attn_wv': _L0_attn_in['wv'], 'L0_attn_wo': _L0_attn_in['wo'], 'L0_ffn_W': _L0_ffn_in['W'], 'L0_ffn_bias': _L0_ffn_in['bias'], 'L0_ffn_A': _L0_ffn_in['A'], 'L0_ffn_Bf': _L0_ffn_in['Bf'], 'L0_ffn_coeffs': _L0_ffn_in['coeffs'], 'L0_ffn_scales': _L0_ffn_in['scales']}

def reference(x, L0_tok_log_dt, L0_tok_B, L0_tok_inv_A_real, L0_tok_A_imag, L0_attn_wq, L0_attn_wk, L0_attn_wv, L0_attn_wo, L0_ffn_W, L0_ffn_bias, L0_ffn_A, L0_ffn_Bf, L0_ffn_coeffs, L0_ffn_scales):
    import jax
    import jax.numpy as jnp

    def _L0_tok_ref(log_dt, C, B, inv_A_real, A_imag, L):
        import jax, jax.numpy as jnp
        import numpy as np
        H, N, S, CH, LEN = (128, 64, 128, 1, 1024)

        def _s4d_kernel(log_dt, C, B, inv_A_real, A_imag, L):
            dt = jnp.exp(log_dt)
            Cc = C[..., 0] + 1j * C[..., 1]
            Bc = B[..., 0] + 1j * B[..., 1]
            A = -jnp.exp(inv_A_real) + 1j * A_imag
            rep = H // A.shape[0]
            A = jnp.tile(A, (rep, 1))
            Bc = jnp.tile(Bc, (rep, 1))
            dtA = A * dt[:, None]
            Cc = Bc[None, :, :] * Cc
            Cc = Cc * (jnp.exp(dtA) - 1.0) / A
            ell = jnp.arange(L, dtype=jnp.float32)
            V = jnp.exp(dtA[:, :, None] * ell)
            K = 2.0 * jnp.einsum('chn,hnl->chl', Cc, V).real
            return K.astype(jnp.float32)
        return _s4d_kernel(log_dt, C, B, inv_A_real, A_imag, L)

    def _L0_attn_ref(hidden_states, wq, wk, wv, wo):
        import jax, jax.numpy as jnp
        import numpy as np
        import math
        B, S, D = (1, 512, 1024)
        H, KV, HD = (32, 8, 128)
        GROUPS = H // KV
        SYS_LEN, IMG_LEN = (35, 144)
        ENH, SUP = (1.5, 0.5)
        ROPE_BASE = 10000.0

        def _rope_cos_sin(seq_len, dtype):
            inv_freq = 1.0 / ROPE_BASE ** (jnp.arange(0, HD, 2, dtype=jnp.float32) / HD)
            pos = jnp.arange(seq_len, dtype=jnp.float32)
            freqs = pos[:, None] * inv_freq[None, :]
            emb = jnp.concatenate([freqs, freqs], axis=-1)
            return (jnp.cos(emb).astype(dtype), jnp.sin(emb).astype(dtype))

        def _rotate_half(x):
            x1, x2 = (x[..., :HD // 2], x[..., HD // 2:])
            return jnp.concatenate([-x2, x1], axis=-1)
        bsz, q_len, _ = hidden_states.shape
        dt = hidden_states.dtype
        q = (hidden_states @ wq.T).reshape(bsz, q_len, H, HD).transpose(0, 2, 1, 3)
        k = (hidden_states @ wk.T).reshape(bsz, q_len, KV, HD).transpose(0, 2, 1, 3)
        v = (hidden_states @ wv.T).reshape(bsz, q_len, KV, HD).transpose(0, 2, 1, 3)
        cos, sin = _rope_cos_sin(q_len, dt)
        q = q * cos + _rotate_half(q) * sin
        k = k * cos + _rotate_half(k) * sin
        k = jnp.repeat(k, GROUPS, axis=1)
        v = jnp.repeat(v, GROUPS, axis=1)
        scores = jnp.einsum('bhqd,bhkd->bhqk', q, k) / math.sqrt(HD)
        kpos = jnp.arange(q_len)
        key_scale = jnp.where(kpos < SYS_LEN, SUP, jnp.where(kpos < SYS_LEN + IMG_LEN, ENH, 1.0)).astype(dt)
        qpos = jnp.arange(q_len)
        row_sel = (qpos >= SYS_LEN + IMG_LEN)[:, None]
        scale = jnp.where(row_sel, key_scale[None, :], jnp.ones((), dt))
        scores = scores * scale
        causal = jnp.where(qpos[:, None] >= kpos[None, :], 0.0, jnp.finfo(jnp.float32).min)
        scores = scores + causal.astype(dt)
        probs = jax.nn.softmax(scores.astype(jnp.float32), axis=-1).astype(dt)
        attn = jnp.einsum('bhqk,bhkd->bhqd', probs, v)
        attn = attn.transpose(0, 2, 1, 3).reshape(bsz, q_len, H * HD)
        return attn @ wo.T

    def _L0_ffn_ref(x, W, bias, A, Bf, coeffs, scales):
        import jax, jax.numpy as jnp
        import numpy as np
        out = jnp.einsum('bsd,od->bso', x, W) + bias
        xa = jnp.einsum('bsd,erd->ebsr', x, A)
        w = coeffs * scales
        upd = jnp.einsum('ebsr,eor,e->bso', xa, Bf, w)
        return out + upd
    h = _L0_tok_ref(L0_tok_log_dt, x, L0_tok_B, L0_tok_inv_A_real, L0_tok_A_imag, 1024)
    h = h + _L0_attn_ref(_layernorm(h, axis=-1), L0_attn_wq, L0_attn_wk, L0_attn_wv, L0_attn_wo)
    h = h + _L0_ffn_ref(_layernorm(h, axis=-1), L0_ffn_W, L0_ffn_bias, L0_ffn_A, L0_ffn_Bf, L0_ffn_coeffs, L0_ffn_scales)
    return h

_drawn_inputs = setup_inputs


def setup_inputs(seed=0):
    import zlib

    import numpy as np

    out = dict(_drawn_inputs(seed))
    spreads = {'L0_tok_inv_A_real': (-0.6931471824645996, 0.2), 'L0_ffn_scales': (0.5, 0.6)}
    factors = {}
    for name, (base, spread) in spreads.items():
        noise = np.random.default_rng([zlib.crc32(name.encode()), seed]).standard_normal(out[name].shape)
        drawn = base * np.exp(spread * noise) if base else spread * noise
        out[name] = jnp.asarray(drawn.astype(out[name].dtype))
    for name, factor in factors.items():
        out[name] = (out[name] * factor).astype(out[name].dtype)
    return out
```

```python
import math
from contextlib import ExitStack

import numpy as np

import concourse.bass as bass
from concourse import mybir

F32 = mybir.dt.float32
F32R = mybir.dt.float32r
I32 = mybir.dt.int32
ALU = mybir.AluOpType
ACT = mybir.ActivationFunctionType

NB, SEQ, NS = 16, 128, 64
D = 1024
A8, P = D // 128, 128
HD, NKV, GQ = 128, 8, 4
TT = 4
NT = NB * SEQ // TT
CPT = NT // SEQ
QSCALE = 1.0 / math.sqrt(HD)
EPS = 1e-5
ER = 256

W_TT = 10 * NKV + 8
M_TT = 14 * NKV + 8
U_TT = 4 * NKV
NSLOT = 4

B0, B1 = 16, 8
NTAB = B0 + B1 + A8
HBLK = 8
MAGIC = 12582912.0
TWO_PI_LOW = 6.283185


def s4d_and_lora_fold(nc, ins, h_dram, weff_dram):
    ctx = ExitStack()
    with ctx:
        def sb(name, shape, dt=F32):
            return ctx.enter_context(nc.sbuf_tensor(name, shape, dt))

        def sem(name):
            return ctx.enter_context(nc.semaphore(name))

        small = sb("small", [P, 5, SEQ])
        tab = sb("tab", [P, NTAB])
        coef = sb("coef", [P, 2, SEQ, NB])
        hbuf = sb("hbuf", [P, A8, NB, SEQ])
        flat = hbuf[:].rearrange("p a c s -> p (a c s)")

        def big(i):
            return flat[:, i * SEQ * NTAB:(i + 1) * SEQ * NTAB].rearrange("p (s j) -> p s j", j=NTAB)

        turn, absturn, decay, mag = big(0), big(1), big(2), big(3)
        cosr = sb("cosr", [P, SEQ, NTAB])
        sini = sb("sini", [P, SEQ, NTAB])
        x0 = sb("x0", [P, SEQ, B0])
        y0 = sb("y0", [P, SEQ, B0])
        wa = sb("wa", [P, SEQ, A8])
        wb = sb("wb", [P, SEQ, A8])
        w2a = sb("w2a", [P, 2, HBLK, P])
        w2b = sb("w2b", [P, 2, HBLK, P])
        pa = sb("pa", [P, 2, HBLK, P])
        pb = sb("pb", [P, 2, HBLK, P])
        ex = sb("ex", [P, 2, SEQ])
        t = sb("t", [P, 8, SEQ])
        ti = sb("ti", [P, 2, SEQ], I32)
        half_pi = sb("half_pi", [P, 1])
        lora_a = sb("lora_a", [P, 2, D])
        lora_b = sb("lora_b", [P, 2, D])
        lora_w = sb("lora_w", [P, 4])
        lora_wt = sb("lora_wt", [P, 2, 512])
        lora_out = sb("lora_out", [P, 2, 512])
        ident = sb("ident1", [P, P])
        banks = [ctx.enter_context(nc.psum_tensor(f"s4d{i}", [P, 512], F32)) for i in range(8)]

        in_small, in_coef = sem("in_small"), sem("in_coef")
        in_lora = sem("in_lora")
        in_wt = [sem(f"in_wt{i}") for i in range(2)]
        dve_done = sem("dve_done")
        act_done = sem("act_done")
        lora_b_ready = sem("lora_b_ready")
        lora_ready, lora_read = sem("lora_ready"), sem("lora_read")
        lora_stored = [sem(f"lora_stored{i}") for i in range(2)]
        w2_mul, blk_ready, blk_used, h_read = sem("w2_mul"), sem("blk_ready"), sem("blk_used"), sem("h_read")
        h_stored = sem("h_stored")
        NBLK = SEQ // HBLK
        marks = {}
        block = ctx.enter_context(nc.Block())

        @block.sync
        def _(sp):
            sp.dma_start(small[:], ins["small"]).then_inc(in_small, 16)
            sp.dma_start(tab[:], ins["tab"]).then_inc(in_small, 16)
            sp.dma_start(lora_a[:], ins["lora_a"]).then_inc(in_lora, 16)
            sp.dma_start(lora_b[:], ins["lora_b"]).then_inc(in_lora, 16)
            sp.dma_start(lora_w[:], ins["lora_w"]).then_inc(in_lora, 16)
            sp.dma_start(ident[:], ins["ident"]).then_inc(in_lora, 16)
            sp.dma_start(coef[:], ins["coef"]).then_inc(in_coef, 16)

            def load_wt(n):
                a, oh = n // 2, n % 2
                sp.dma_start(lora_wt[:, n % 2, :], ins["wt"][a, :, oh * 512:(oh + 1) * 512]).then_inc(in_wt[n % 2], 16)

            load_wt(0)
            load_wt(1)
            for n in range(16):
                a, oh = n // 2, n % 2
                sp.wait_ge(lora_read, n + 1)
                sp.dma_start(weff_dram[oh * 4:oh * 4 + 4, :, a, :].rearrange("t p o -> p t o"),
                             lora_out[:, n % 2, :].rearrange("p (t o) -> p t o", t=4)).then_inc(lora_stored[n % 2], 16)
                if n + 2 < 16:
                    load_wt(n + 2)
            sp.wait_ge(h_read, SEQ // 4)
            for tt in range(TT):
                sp.dma_start(h_dram[tt], hbuf[:, :, tt * CPT:(tt + 1) * CPT, :]).then_inc(h_stored, 16)
            sp.wait_ge(h_stored, 16 * TT)
            for i in range(2):
                sp.wait_ge(lora_stored[i], 16 * 8)

        @block.vector
        def _(dve):
            n_done = [0]

            def link(ins_):
                n_done[0] += 1
                ins_.then_inc(dve_done, 1)
                dve.wait_ge(dve_done, n_done[0])

            v = nc.vector
            link(v.memset(half_pi[:], math.pi / 2))
            dve.wait_ge(in_lora, 64)
            link(v.tensor_tensor(lora_w[:, 0:2], lora_w[:, 0:2], lora_w[:, 2:4], ALU.mult))
            for k in range(2):
                ins_ = v.tensor_scalar(lora_b[:, k, :], lora_b[:, k, :], lora_w[:, k:k + 1], None, ALU.mult)
                ins_.then_inc(lora_b_ready, 1)
            dve.wait_ge(in_small, 32)
            arg = small[:, 0:2, :]
            k2, r2, e2 = t[:, 0:2, :], t[:, 2:4, :], t[:, 4:6, :]
            link(v.tensor_scalar(k2, arg, 1.4426950408889634, MAGIC, ALU.mult, ALU.add))
            link(v.tensor_scalar(k2, k2, MAGIC, -126.0, ALU.subtract, ALU.max))
            link(v.tensor_scalar(k2, k2, 127.0, None, ALU.min))
            link(v.scalar_tensor_tensor(r2, k2, -0.693359375, arg, ALU.mult, ALU.add))
            link(v.scalar_tensor_tensor(r2, k2, 2.12194440e-4, r2, ALU.mult, ALU.add))
            link(v.tensor_scalar(ti[:], k2, 127.0, 8388608.0, ALU.add, ALU.mult))
            link(v.tensor_scalar(e2, r2, 1.0 / 5040, 1.0 / 720, ALU.mult, ALU.add))
            for c in (1.0 / 120, 1.0 / 24, 1.0 / 6, 0.5, 1.0):
                link(v.tensor_tensor(e2, e2, r2, ALU.mult))
                link(v.tensor_scalar(e2, e2, c, None, ALU.add))
            link(v.tensor_tensor(e2, e2, r2, ALU.mult))
            link(v.tensor_scalar(e2, e2, 1.0, None, ALU.add))
            link(v.tensor_tensor(ex[:], e2, ti[:].bitcast(F32), ALU.mult))
            dt, are = ex[:, 0, :], ex[:, 1, :]
            ar, theta, vturn, kk = t[:, 0, :], t[:, 1, :], t[:, 2, :], t[:, 3, :]
            link(v.scalar_tensor_tensor(ar, are, -1.0, dt, ALU.mult, ALU.mult))
            link(v.tensor_tensor(theta, small[:, 2, :], dt, ALU.mult))
            link(v.tensor_scalar(kk, theta, 1.0 / (2 * math.pi), MAGIC, ALU.mult, ALU.add))
            link(v.tensor_scalar(kk, kk, MAGIC, None, ALU.subtract))
            link(v.scalar_tensor_tensor(vturn, kk, -6.28125, theta, ALU.mult, ALU.add))
            link(v.scalar_tensor_tensor(vturn, kk, -0.0019353071795864769, vturn, ALU.mult, ALU.add))
            link(v.tensor_scalar(vturn, vturn, 1.0 / (2 * math.pi), None, ALU.mult))

            def rows(x):
                return x.unsqueeze(2).broadcast_to([P, SEQ, NTAB])

            tabs = tab[:].unsqueeze(1).broadcast_to([P, SEQ, NTAB])
            link(v.tensor_tensor(decay, rows(ar), tabs, ALU.mult))
            decay_at = n_done[0]
            link(v.tensor_tensor(turn, rows(vturn), tabs, ALU.mult))
            link(v.tensor_scalar(absturn, turn, MAGIC, None, ALU.add))
            link(v.scalar_tensor_tensor(turn, absturn, MAGIC, turn, ALU.subtract, ALU.subtract))
            turn_at = n_done[0]
            link(v.scalar_tensor_tensor(absturn, turn, -1.0, turn, ALU.mult, ALU.max))
            abs_at = n_done[0]
            v.setup_marks = None if False else None
            marks["decay"], marks["turn"], marks["abs"] = decay_at, turn_at, abs_at
            em, lim, mask = t[:, 4, :], t[:, 5, :], ti[:, 0, :]
            link(v.tensor_scalar(lim, ar, -0.5, None, ALU.max))
            link(v.tensor_scalar(em, lim, 1.0 / 40320, 1.0 / 5040, ALU.mult, ALU.add))
            for c in (1.0 / 720, 1.0 / 120, 1.0 / 24, 1.0 / 6, 0.5, 1.0):
                link(v.tensor_tensor(em, em, lim, ALU.mult))
                link(v.tensor_scalar(em, em, c, None, ALU.add))
            link(v.tensor_tensor(em, em, lim, ALU.mult))
            link(v.tensor_scalar(mask, ar, -0.5, None, ALU.is_lt))
            dve.wait_ge(act_done, 4)
            link(v.tensor_scalar(lim, mag[:, :, 1], -1.0, None, ALU.add))
            link(v.copy_predicated(em, mask, lim))
            s1, c1, sh = sini[:, :, 1], cosr[:, :, 1], t[:, 3, :]
            c1m, er, ei = t[:, 5, :], t[:, 6, :], t[:, 7, :]
            link(v.scalar_tensor_tensor(c1m, sh, -2.0, sh, ALU.mult, ALU.mult))
            link(v.tensor_tensor(er, em, c1, ALU.mult))
            link(v.tensor_tensor(er, er, c1m, ALU.add))
            link(v.scalar_tensor_tensor(ei, em, 1.0, s1, ALU.add, ALU.mult))
            aim, den, tmp = small[:, 2, :], t[:, 0, :], t[:, 1, :]
            link(v.tensor_tensor(den, are, are, ALU.mult))
            link(v.tensor_tensor(tmp, aim, aim, ALU.mult))
            link(v.tensor_tensor(den, den, tmp, ALU.add))
            link(v.reciprocal(den, den))
            link(v.tensor_scalar(den, den, 2.0, None, ALU.mult))
            xq, yq = t[:, 2, :], t[:, 3, :]
            link(v.tensor_tensor(xq, ei, aim, ALU.mult))
            link(v.tensor_tensor(tmp, er, are, ALU.mult))
            link(v.tensor_tensor(xq, xq, tmp, ALU.subtract))
            link(v.tensor_tensor(xq, xq, den, ALU.mult))
            link(v.tensor_tensor(yq, ei, are, ALU.mult))
            link(v.tensor_tensor(tmp, er, aim, ALU.mult))
            link(v.tensor_tensor(yq, yq, tmp, ALU.add))
            link(v.scalar_tensor_tensor(yq, yq, -1.0, den, ALU.mult, ALU.mult))
            gr, gi = t[:, 4, :], t[:, 5, :]
            br, bi = small[:, 3, :], small[:, 4, :]
            link(v.tensor_tensor(gr, xq, br, ALU.mult))
            link(v.tensor_tensor(tmp, yq, bi, ALU.mult))
            link(v.tensor_tensor(gr, gr, tmp, ALU.subtract))
            link(v.tensor_tensor(gi, xq, bi, ALU.mult))
            link(v.tensor_tensor(tmp, yq, br, ALU.mult))
            link(v.tensor_tensor(gi, gi, tmp, ALU.add))
            link(v.tensor_tensor(cosr[:], cosr[:], mag, ALU.mult))
            link(v.tensor_tensor(sini[:], sini[:], mag, ALU.mult))
            hr, hi = slice(0, 64), slice(64, 128)
            link(v.tensor_copy(x0[hr], cosr[hr, :, 0:B0]))
            link(v.tensor_copy(x0[hi], sini[hi, :, 0:B0]))
            link(v.tensor_scalar(y0[hr], sini[hr, :, 0:B0], -1.0, None, ALU.mult))
            link(v.tensor_copy(y0[hi], cosr[hi, :, 0:B0]))

            def eight(x):
                return x.unsqueeze(2).broadcast_to([P, SEQ, A8])

            rot, iot = cosr[:, :, B0 + B1:NTAB], sini[:, :, B0 + B1:NTAB]

            def scratch(x):
                return x[:, 0].rearrange("p s q -> p (s q)").rearrange("p (s a) -> p s a", a=A8)

            grr, gii, tm = scratch(pa), scratch(pb), scratch(w2a)
            link(v.tensor_tensor(grr, rot, eight(gr), ALU.mult))
            link(v.tensor_tensor(tm, iot, eight(gi), ALU.mult))
            link(v.tensor_tensor(grr, grr, tm, ALU.subtract))
            link(v.tensor_tensor(gii, rot, eight(gi), ALU.mult))
            link(v.tensor_tensor(tm, iot, eight(gr), ALU.mult))
            link(v.tensor_tensor(gii, gii, tm, ALU.add))
            link(v.tensor_copy(wa[hr], grr[hr]))
            link(v.tensor_scalar(wa[hi], gii[hi], -1.0, None, ALU.mult))
            link(v.tensor_scalar(wb[hr], gii[hr], -1.0, None, ALU.mult))
            link(v.tensor_scalar(wb[hi], grr[hi], -1.0, None, ALU.mult))
            dve.wait_ge(in_coef, 16)

            for n in range(NBLK):
                s0, s1_ = n * HBLK, (n + 1) * HBLK
                d = n % 2
                if n >= 2:
                    dve.wait_ge(blk_used, n - 1)

                def b_of(x, lo, cnt, inner):
                    y = x[:, s0:s1_, lo:lo + cnt]
                    return (y.unsqueeze(3).broadcast_to([P, HBLK, cnt, inner]))

                def mid(x, outer, cnt):
                    return x[:, s0:s1_, 0:cnt].unsqueeze(2).broadcast_to([P, HBLK, outer, cnt])

                def out4(x, outer):
                    return x[:, d].rearrange("p s (o i) -> p s o i", o=outer)

                v.tensor_tensor(out4(w2a, B1), b_of(cosr, B0, B1, B0), mid(x0, B1, B0), ALU.mult)
                v.tensor_tensor(out4(w2b, B1), b_of(sini, B0, B1, B0), mid(y0, B1, B0), ALU.mult).then_inc(w2_mul, 1)
                v.tensor_tensor(out4(pa, NB), b_of(coef[:, 0], 0, NB, A8), mid(wa, NB, A8), ALU.mult)
                v.tensor_tensor(out4(pb, NB), b_of(coef[:, 1], 0, NB, A8), mid(wb, NB, A8), ALU.mult)
                dve.wait_ge(w2_mul, n + 1)
                v.tensor_tensor(w2a[:, d], w2a[:, d], w2b[:, d], ALU.add).then_inc(blk_ready, 1)

        @block.scalar
        def _(act):
            act.wait_ge(dve_done, marks["decay"])
            nc.scalar.activation(mag, decay, ACT.Exp).then_inc(act_done, 1)
            act.wait_ge(dve_done, marks["turn"])
            nc.scalar.activation(sini[:], turn, ACT.Sin, scale=-TWO_PI_LOW).then_inc(act_done, 1)
            act.wait_ge(dve_done, marks["abs"])
            nc.scalar.activation(cosr[:], absturn, ACT.Sin, bias=half_pi[:], scale=-TWO_PI_LOW).then_inc(act_done, 1)
            nc.scalar.activation(t[:, 3, :], turn[:, :, 1], ACT.Sin, scale=TWO_PI_LOW / 2).then_inc(act_done, 1)
            for n in range(16):
                act.wait_ge(lora_ready, n + 1)
                if n >= 2:
                    act.wait_ge(lora_stored[n % 2], 16 * (n // 2))
                nc.scalar.activation(lora_out[:, n % 2, :], banks[n % 2][:], ACT.Copy).then_inc(lora_read, 1)
            for n in range(SEQ // 4):
                act.wait_ge(blk_used, n // 2 + 1)
                nc.scalar.activation(hbuf[:, :, :, 4 * n:4 * n + 4].rearrange("p a c s -> p s c a"),
                                     banks[2 + n % 6][:].rearrange("p (s c a) -> p s c a", s=4, a=A8),
                                     ACT.Copy).then_inc(h_read, 1)

        @block.tensor
        def _(pe):
            pe.wait_ge(in_lora, 64)
            pe.wait_ge(lora_b_ready, 2)
            for n in range(16):
                a, oh = n // 2, n % 2
                pe.wait_ge(in_wt[n % 2], 16 * (n // 2 + 1))
                if n >= 2:
                    pe.wait_ge(lora_read, n - 1)
                for k in range(2):
                    nc.tensor.matmul(banks[n % 2][:], lora_a[:, k, a * P:(a + 1) * P],
                                     lora_b[:, k, oh * 512:(oh + 1) * 512], start=(k == 0), stop=False)
                nc.tensor.matmul(banks[n % 2][:], ident[:], lora_wt[:, n % 2, :],
                                 start=False, stop=True).then_inc(lora_ready, 1)
            for n in range(NBLK):
                pe.wait_ge(blk_ready, n + 1)
                for half in range(2):
                    m = 2 * n + half
                    if m >= 6:
                        pe.wait_ge(h_read, m - 5)
                    for j in range(4):
                        s = half * 4 + j
                        out = banks[2 + m % 6][:, j * P:(j + 1) * P]
                        nc.tensor.matmul(out, w2a[:, n % 2, s, :], pa[:, n % 2, s, :], start=True, stop=False)
                        last = nc.tensor.matmul(out, w2a[:, n % 2, s, :], pb[:, n % 2, s, :], start=False, stop=True)
                last.then_inc(blk_used, 1)


def at(tt, total, *terms):
    value = tt * total
    for term in terms:
        value = value + (term[0] * term[1] if isinstance(term, tuple) else term)
    return value


class Step:

    def __init__(self, tt, it, q):
        self.tt, self.it, self.q = tt, it, q
        self.new, self.old = 1 - q, q

    def g(self):
        return self.it * 2 + (1 + self.q)

    def tile(self, j):
        return at(self.tt, W_TT, (20, self.it), 6 + 10 * self.q + j)

    def tile_slot(self, j):
        return (6 + 10 * self.q + j) % NSLOT

    def chunk(self, m):
        return at(self.tt, M_TT, (28, self.it), 6 + 14 * self.q + m)

    def bank(self, m):
        return (6 + 14 * self.q + m) % NSLOT

    def unit(self, u):
        return at(self.tt, U_TT, (8, self.it), 4 * self.q + u)

    def raw_uses(self, j):
        return at(self.tt, W_TT // NSLOT, (20 // NSLOT, self.it), (6 + 10 * self.q + j) // NSLOT + 1)

    def slot_free(self, j):
        return self.chunk(j - 3 if j < 10 else 8 + 2 * (j - 10))

    def heads(self):
        return at(self.tt, NKV, (2, self.it), 1 + self.q)


class First(Step):

    def __init__(self, tt):
        self.tt, self.new = tt, 0

    def tile(self, j):
        return at(self.tt, W_TT, j)

    def tile_slot(self, j):
        return j % NSLOT

    def raw_uses(self, j):
        return at(self.tt, W_TT // NSLOT, j // NSLOT + 1)

    def slot_free(self, j):
        return self.chunk(j - 3) if j > 3 else None

    def chunk(self, m):
        return at(self.tt, M_TT, m)

    def bank(self, m):
        return m % NSLOT

    def heads(self):
        return at(self.tt, NKV, 0)


class Last(Step):

    def __init__(self, tt):
        super().__init__(tt, 3, 1)

    def tile(self, j):
        return at(self.tt, W_TT, 70 + j)

    def tile_slot(self, j):
        return (70 + j) % NSLOT

    def raw_uses(self, j):
        return at(self.tt, W_TT // NSLOT, (70 + j) // NSLOT + 1)

    def slot_free(self, j):
        return self.chunk(2 * (j - 6) if j < 10 else 8 + 2 * (j - 10) if j < 14 else j + 1)

    def chunk(self, m):
        return at(self.tt, M_TT, 98 + m)

    def bank(self, m):
        return (98 + m) % NSLOT


def transformer(nc, ins, h_dram, weff_dram, out_dram):
    ctx = ExitStack()
    with ctx:
        def sb(name, shape, dt=F32):
            return ctx.enter_context(nc.sbuf_tensor(name, shape, dt))

        def sem(name):
            return ctx.enter_context(nc.semaphore(name))

        cos, sin = sb("cos", [P, SEQ]), sb("sin", [P, SEQ])
        mask = sb("mask", [P, SEQ])
        ident = sb("ident2", [P, P])
        mean_w = sb("mean_w", [P, P])
        bias = sb("bias", [P, A8])
        acc = sb("acc", [P, A8, NT])
        dev = sb("dev", [P, A8, NT])
        sq = sb("sq", [P, 2, NT])
        rstd = sb("rstd", [P, NT])
        xh, xl = sb("xh", [P, A8, NT], F32R), sb("xl", [P, A8, NT], F32R)
        raw = sb("raw", [P, NSLOT, D])
        wh, wl = sb("wh", [P, NSLOT, D], F32R), sb("wl", [P, NSLOT, D], F32R)
        qh, ql = sb("qh", [P, 2, GQ, NT], F32R), sb("ql", [P, 2, GQ, NT], F32R)
        kh, kl = sb("kh", [P, 2, NT], F32R), sb("kl", [P, 2, NT], F32R)
        vh, vl = sb("vh", [P, 2, NT], F32R), sb("vl", [P, 2, NT], F32R)
        vt = sb("vt", [P, NT])
        rot, direct, roped = sb("rot", [P, NT]), sb("direct", [P, NT]), sb("roped", [P, NT])
        prob = sb("prob", [P, 2, GQ, SEQ])
        stat = sb("stat", [P, 2, 3, GQ])
        pth, ptl = sb("pth", [P, 2, NT], F32R), sb("ptl", [P, 2, NT], F32R)
        oh, ol = sb("oh", [P, GQ, NT], F32R), sb("ol", [P, GQ, NT], F32R)

        chunk_ps = [ctx.enter_context(nc.psum_tensor(f"chunk{i}", [P, NT], F32)) for i in range(NSLOT)]
        score_ps = [ctx.enter_context(nc.psum_tensor(f"score{i}", [P, NT], F32)) for i in range(2)]
        turn_ps = ctx.enter_context(nc.psum_tensor("turn", [P, NT], F32))
        attn_ps = ctx.enter_context(nc.psum_tensor("attn", [P, NT], F32))

        in_const = sem("in_const")
        in_h = sem("in_h")
        raw_in = [sem(f"raw_in{i}") for i in range(NSLOT)]
        out_done = sem("out_done")
        w_hi = sem("w_hi")
        w_lo = sem("w_lo")
        chunk_ready, chunk_free = sem("chunk_ready"), sem("chunk_free")
        mean_ready, dev_ready, sq_ready = sem("mean_ready"), sem("dev_ready"), sem("sq_ready")
        var_step, var_ready = sem("var_step"), sem("var_ready")
        rstd_step, std_ready = sem("rstd_step"), sem("std_ready")
        norm_ready, x_hi, x_lo = sem("norm_ready"), sem("x_hi"), sem("x_lo")
        rot_ready, rope_step, rope_ready = sem("rot_ready"), sem("rope_step"), sem("rope_ready")
        r_hi, r_lo = sem("r_hi"), sem("r_lo")
        turn_ready, turn_free = sem("turn_ready"), sem("turn_free")
        v_hi = sem("v_hi")
        score_ready, score_free = sem("score_ready"), sem("score_free")
        max_step, max_ready, exp_ready = sem("max_step"), sem("max_ready"), sem("exp_ready")
        inv_step, prob_ready = sem("inv_step"), sem("prob_ready")
        pt_hi = sem("pt_hi")
        attn_ready, attn_free = sem("attn_ready"), sem("attn_free")
        o_hi = sem("o_hi")

        block = ctx.enter_context(nc.Block())

        @block.sync
        def _(sp):
            for name, dst in (("cos", cos), ("sin", sin), ("mask", mask), ("ident", ident),
                              ("mean_w", mean_w), ("bias", bias)):
                sp.dma_start(dst[:], ins[name]).then_inc(in_const, 16)

            def load(st, j, src):
                sp.wait_ge(w_lo, st.tile(j) + 1)
                sp.dma_start(raw[:, st.tile_slot(j), :], src).then_inc(raw_in[st.tile_slot(j)], 16)

            sp.sem_inc(out_done, 16)
            with sp.Fori(0, TT) as tt:
                sp.wait_ge(out_done, tt * (16 * A8) + 16)
                sp.dma_start(acc[:].rearrange("p a (c s) -> p a c s", c=CPT), h_dram[tt]).then_inc(in_h, 16)
                first, last = First(tt), Last(tt)
                for j in range(6):
                    load(first, j, ins["wqkv"][0, j])

                def step_loads(st):
                    for j in range(6):
                        load(st, j, ins["wqkv"][st.g(), j])
                    for j in range(4):
                        load(st, 6 + j, ins["wo"][st.g() - 1, j])

                with sp.Fori(0, 3) as it:
                    for q in range(2):
                        step_loads(Step(tt, it, q))
                step_loads(Step(tt, 3, 0))
                for j in range(4):
                    load(last, 6 + j, ins["wo"][NKV - 1, j])
                for j in range(8):
                    load(last, 10 + j, weff_dram[j].rearrange("p a o -> p (a o)"))
                for o in range(A8):
                    sp.wait_ge(chunk_free, last.chunk(14 + o) + (NSLOT + 1))
                    sp.dma_start(out_dram[tt, o], acc[:, o, :]).then_inc(out_done, 16)
            sp.wait_ge(out_done, 16 * A8 * TT + 16)

        @block.tensor
        def _(pe):
            mm = nc.tensor.matmul

            def three(out, wah, wal, bh, bl, start, stop):
                mm(out, wah, bh, start=start, stop=False)
                mm(out, wah, bl, start=False, stop=False)
                return mm(out, wal, bh, start=False, stop=stop)

            def layer_norm(tt, which):
                pe.wait_ge(score_free, tt * U_TT + (2 + U_TT * which))
                if which == 0:
                    pe.wait_ge(in_h, tt * 16 + 16)
                else:
                    pe.wait_ge(chunk_free, tt * M_TT + (NSLOT + 14 * NKV))
                for a in range(A8):
                    last = mm(score_ps[0][:], mean_w[:], acc[:, a, :], start=(a == 0), stop=(a == A8 - 1))
                last.then_inc(mean_ready, 1)
                for a in range(A8):
                    pe.wait_ge(sq_ready, tt * 16 + (8 * which + a + 1))
                    last = mm(score_ps[1][:], mean_w[:], sq[:, a % 2, :], start=(a == 0), stop=(a == A8 - 1))
                    last.then_inc(var_step, 1)

            def project(st, j, x_count=None):
                pe.wait_ge(chunk_free, st.chunk(j) + 1)
                pe.wait_ge(w_lo, st.tile(j) + (NSLOT + 1))
                slot = st.tile_slot(j)
                for a in range(A8):
                    if x_count is not None:
                        pe.wait_ge(x_lo, x_count + (a + 1))
                    w = slice(a * P, (a + 1) * P)
                    last = three(chunk_ps[st.bank(j)][:], wh[:, slot, w], wl[:, slot, w],
                                 xh[:, a, :], xl[:, a, :], a == 0, a == A8 - 1)
                last.then_inc(chunk_ready, 1)

            def turn_v(st):
                pe.wait_ge(chunk_free, st.chunk(1) + (NSLOT + 1))
                pe.wait_ge(turn_free, st.heads() * 5 + 1)
                for u in range(CPT):
                    last = nc.tensor.transpose(turn_ps[:, u * P:(u + 1) * P], vt[:, u * P:(u + 1) * P], ident[:])
                last.then_inc(turn_ready, 1)

            def scores(st, u):
                if u == 0:
                    pe.wait_ge(r_lo, st.heads() * 5)
                pe.wait_ge(score_free, st.unit(u) + 1)
                tok = slice(u * SEQ, (u + 1) * SEQ)
                for h in range(GQ):
                    last = three(score_ps[u % 2][:, h * SEQ:(h + 1) * SEQ],
                                 qh[:, st.old, h, tok], ql[:, st.old, h, tok],
                                 kh[:, st.old, tok], kl[:, st.old, tok], True, True)
                last.then_inc(score_ready, 1)

            def turn_probs(st, u):
                pe.wait_ge(prob_ready, st.unit(u) + 1)
                pe.wait_ge(turn_free, st.heads() * 5 + (u - 3))
                for h in range(GQ):
                    last = nc.tensor.transpose(turn_ps[:, h * P:(h + 1) * P], prob[:, u % 2, h, :], ident[:])
                last.then_inc(turn_ready, 1)

            def attend(st, u):
                pe.wait_ge(turn_free, st.heads() * 5 + (u - 2))
                pe.wait_ge(attn_free, st.unit(u) + 1)
                keys = slice(u * P, (u + 1) * P)
                three(attn_ps[:], vh[:, st.old, keys], vl[:, st.old, keys],
                      pth[:, u % 2, :], ptl[:, u % 2, :], True, True).then_inc(attn_ready, 1)

            def wo_chunks(st):
                for o in range(A8):
                    pe.wait_ge(chunk_free, st.chunk(6 + o) + 1)
                    if o == 0:
                        pe.wait_ge(attn_free, st.unit(3) + 2)
                    slot = st.tile_slot(6 + o // 2)
                    if o % 2 == 0:
                        pe.wait_ge(w_lo, st.tile(6 + o // 2) + (NSLOT + 1))
                    for h in range(GQ):
                        w = slice(h * 256 + (o % 2) * P, h * 256 + (o % 2) * P + P)
                        last = three(chunk_ps[st.bank(6 + o)][:], wh[:, slot, w], wl[:, slot, w],
                                     oh[:, h, :], ol[:, h, :], h == 0, h == GQ - 1)
                    last.then_inc(chunk_ready, 1)

            def step(st):
                scores(st, 0)
                project(st, 0)
                scores(st, 1)
                turn_probs(st, 0)
                project(st, 1)
                attend(st, 0)
                scores(st, 2)
                turn_probs(st, 1)
                project(st, 2)
                attend(st, 1)
                scores(st, 3)
                turn_probs(st, 2)
                project(st, 3)
                attend(st, 2)
                turn_probs(st, 3)
                project(st, 4)
                attend(st, 3)
                project(st, 5)
                turn_v(st)
                wo_chunks(st)

            pe.wait_ge(in_const, 16 * 6)
            with pe.Fori(0, TT) as tt:
                layer_norm(tt, 0)
                first, last = First(tt), Last(tt)
                for j in range(6):
                    project(first, j, tt * 16 if j == 0 else None)
                turn_v(first)
                with pe.Fori(0, 3) as it:
                    for q in range(2):
                        step(Step(tt, it, q))
                step(Step(tt, 3, 0))
                scores(last, 0)
                scores(last, 1)
                turn_probs(last, 0)
                attend(last, 0)
                scores(last, 2)
                turn_probs(last, 1)
                attend(last, 1)
                scores(last, 3)
                turn_probs(last, 2)
                attend(last, 2)
                turn_probs(last, 3)
                attend(last, 3)
                wo_chunks(last)
                layer_norm(tt, 1)
                for o in range(A8):
                    project_ffn = 14 + o
                    pe.wait_ge(chunk_free, last.chunk(project_ffn) + 1)
                    pe.wait_ge(w_lo, last.tile(10 + o) + (NSLOT + 1))
                    slot = last.tile_slot(10 + o)
                    for a in range(A8):
                        if o == 0:
                            pe.wait_ge(x_lo, tt * 16 + (8 + a + 1))
                        w = slice(a * P, (a + 1) * P)
                        end = three(chunk_ps[last.bank(project_ffn)][:], wh[:, slot, w], wl[:, slot, w],
                                    xh[:, a, :], xl[:, a, :], a == 0, a == A8 - 1)
                    end.then_inc(chunk_ready, 1)

        @block.scalar
        def _(act):
            def split_hi(dst, src, done):
                nc.scalar.activation(dst, src, ACT.Copy).then_inc(done, 1)

            def weights(st, j):
                if st.slot_free(j) is not None:
                    act.wait_ge(chunk_ready, st.slot_free(j))
                slot = st.tile_slot(j)
                act.wait_ge(raw_in[slot], st.raw_uses(j) * 16)
                split_hi(wh[:, slot, :], raw[:, slot, :], w_hi)

            def layer_norm(tt, which):
                base = tt * 16 + 8 * which
                for a in range(A8):
                    act.wait_ge(dev_ready, base + (a + 1))
                    if a >= 2:
                        act.wait_ge(var_step, base + (a - 1))
                    nc.scalar.activation(sq[:, a % 2, :], dev[:, a, :], ACT.Square).then_inc(sq_ready, 1)
                act.wait_ge(rstd_step, tt * 4 + (2 * which + 1))
                nc.scalar.activation(rstd[:], rstd[:], ACT.Sqrt).then_inc(std_ready, 1)
                for a in range(A8):
                    act.wait_ge(norm_ready, base + (a + 1))
                    split_hi(xh[:, a, :], dev[:, a, :], x_hi)

            def rotate(st, j, m):
                act.wait_ge(chunk_ready, st.chunk(j) + 1)
                ps = chunk_ps[st.bank(j)]
                nc.scalar.activation(rot[0:64, :], ps[64:128, :], ACT.Copy)
                nc.scalar.activation(rot[64:128, :], ps[0:64, :], ACT.Copy).then_inc(rot_ready, 1)

            def rope_hi(st, j, m):
                act.wait_ge(rope_ready, st.heads() * 5 + (m + 1))
                dst = kh[:, st.new, :] if j == 0 else qh[:, st.new, j - 2, :]
                split_hi(dst, roped[:], r_hi)

            def v_split(st):
                act.wait_ge(turn_ready, st.heads() * 5 + 1)
                split_hi(vh[:, st.new, :], turn_ps[:], v_hi)

            def exps(st, u):
                act.wait_ge(max_ready, st.unit(u) + 1)
                for h in range(GQ):
                    x = prob[:, u % 2, h, :]
                    last = nc.scalar.activation(x, x, ACT.Exp, bias=stat[:, u % 2, 0, h:h + 1], scale=QSCALE,
                                                accum_out=stat[:, u % 2, 1, h:h + 1])
                last.then_inc(exp_ready, 1)

            def probs_hi(st, u):
                act.wait_ge(turn_ready, st.heads() * 5 + (u - 3))
                split_hi(pth[:, u % 2, :], turn_ps[:], pt_hi)

            def attn_hi(st, u):
                act.wait_ge(attn_ready, st.unit(u) + 1)
                if u == 0:
                    act.wait_ge(chunk_ready, st.chunk(0))
                split_hi(oh[:, :, u * SEQ:(u + 1) * SEQ],
                         attn_ps[:].rearrange("p (h s) -> p h s", h=GQ), o_hi)

            def step(st, nxt):
                weights(*nxt(3))
                exps(st, 0)
                rotate(st, 0, 0)
                probs_hi(st, 0)
                exps(st, 1)
                weights(*nxt(4))
                rope_hi(st, 0, 0)
                probs_hi(st, 1)
                attn_hi(st, 0)
                exps(st, 2)
                weights(*nxt(5))
                rotate(st, 2, 1)
                probs_hi(st, 2)
                attn_hi(st, 1)
                exps(st, 3)
                weights(*nxt(6))
                rope_hi(st, 2, 1)
                rotate(st, 3, 2)
                probs_hi(st, 3)
                attn_hi(st, 2)
                weights(*nxt(7))
                rope_hi(st, 3, 2)
                rotate(st, 4, 3)
                attn_hi(st, 3)
                weights(*nxt(8))
                rope_hi(st, 4, 3)
                v_split(st)
                rotate(st, 5, 4)
                weights(*nxt(9))
                rope_hi(st, 5, 4)
                weights(*nxt(10))
                weights(*nxt(11))
                weights(*nxt(12))

            with act.Fori(0, TT) as tt:
                first, last = First(tt), Last(tt)
                for j in range(3):
                    weights(first, j)
                layer_norm(tt, 0)
                s1 = Step(tt, 0, 0)
                for j in range(6):
                    weights(*((first, j + 3) if j < 3 else (s1, j - 3)))
                    if j >= 1 and j - 1 != 1:
                        m = (0, None, 1, 2, 3, 4)[j - 1]
                        rotate(first, j - 1, m)
                        rope_hi(first, j - 1, m)
                rotate(first, 5, 4)
                v_split(first)
                rope_hi(first, 5, 4)
                with act.Fori(0, 3) as it:
                    for q in range(2):
                        st = Step(tt, it, q)
                        step(st, lambda j: (st, j))
                st = Step(tt, 3, 0)
                step(st, lambda j: (st, j) if j < 10 else (last, j - 4))
                exps(last, 0)
                probs_hi(last, 0)
                exps(last, 1)
                probs_hi(last, 1)
                attn_hi(last, 0)
                exps(last, 2)
                probs_hi(last, 2)
                attn_hi(last, 1)
                exps(last, 3)
                probs_hi(last, 3)
                attn_hi(last, 2)
                attn_hi(last, 3)
                for j in range(9, 13):
                    weights(last, j)
                layer_norm(tt, 1)
                for j in range(13, 18):
                    weights(last, j)

        @block.vector
        def _(dve):
            v = nc.vector

            def split_lo(dst, src, hi, done):
                v.tensor_tensor(dst, src, hi.bitcast(F32), ALU.subtract).then_inc(done, 1)

            def weights(st, j):
                slot = st.tile_slot(j)
                dve.wait_ge(w_hi, st.tile(j) + 1)
                v.tensor_tensor(wl[:, slot, :], raw[:, slot, :], wh[:, slot, :].bitcast(F32),
                                ALU.subtract).then_inc(w_lo, 1)

            def layer_norm(tt, which):
                base = tt * 16 + 8 * which
                dve.wait_ge(mean_ready, tt * 2 + (1 + which))
                for a in range(A8):
                    v.tensor_tensor(dev[:, a, :], acc[:, a, :], score_ps[0][:], ALU.subtract).then_inc(dev_ready, 1)
                dve.wait_ge(var_step, base + 8)
                v.tensor_scalar(rstd[:], score_ps[1][:], EPS, None, ALU.add).then_inc(rstd_step, 1)
                dve.wait_ge(std_ready, tt * 2 + (1 + which))
                v.reciprocal(rstd[:], rstd[:]).then_inc(rstd_step, 1)
                dve.wait_ge(rstd_step, tt * 4 + (2 * which + 2))
                for a in range(A8):
                    v.tensor_tensor(dev[:, a, :], dev[:, a, :], rstd[:], ALU.mult).then_inc(norm_ready, 1)
                    if a >= 1:
                        lo_x(base, a - 1)
                lo_x(base, A8 - 1)

            def lo_x(base, a):
                dve.wait_ge(x_hi, base + (a + 1))
                split_lo(xl[:, a, :], dev[:, a, :], xh[:, a, :], x_lo)

            def rope(st, j, m):
                tab = [P, CPT, SEQ]

                def seqs(x):
                    return x.rearrange("p (c s) -> p c s", c=CPT)

                def table(x):
                    return x[:].unsqueeze(1).broadcast_to(tab)

                dve.wait_ge(rot_ready, st.heads() * 5 + (m + 1))
                v.tensor_tensor(seqs(direct[:]), seqs(chunk_ps[st.bank(j)][:]), table(cos), ALU.mult)
                v.tensor_tensor(seqs(rot[:]), seqs(rot[:]), table(sin), ALU.mult).then_inc(chunk_free, 1)
                dve.wait_ge(chunk_free, st.chunk(j) + (NSLOT + 1))
                v.tensor_tensor(roped[:], direct[:], rot[:], ALU.add).then_inc(rope_ready, 1)

            def rope_lo(st, j, m):
                dve.wait_ge(r_hi, st.heads() * 5 + (m + 1))
                hi, lo = (x[:, st.new, :] if j == 0 else y[:, st.new, j - 2, :] for x, y in ((kh, qh), (kl, ql)))
                split_lo(lo, roped[:], hi, r_lo)

            def v_copy(st):
                dve.wait_ge(chunk_ready, st.chunk(1) + 1)
                v.tensor_copy(vt[:], chunk_ps[st.bank(1)][:]).then_inc(chunk_free, 1)

            def v_split(st):
                dve.wait_ge(v_hi, st.heads() + 1)
                split_lo(vl[:, st.new, :], turn_ps[:], vh[:, st.new, :], turn_free)

            def maxima(st, u):
                dve.wait_ge(score_ready, st.unit(u) + 1)
                v.tensor_tensor(prob[:, u % 2], score_ps[u % 2][:].rearrange("p (h s) -> p h s", h=GQ),
                                mask[:].unsqueeze(1).broadcast_to([P, GQ, SEQ]), ALU.add).then_inc(score_free, 1)
                dve.wait_ge(score_free, st.unit(u) + 3)
                v.reduce_max(stat[:, u % 2, 0, :], prob[:, u % 2], mybir.AxisListType.X).then_inc(max_step, 1)
                dve.wait_ge(max_step, st.unit(u) + 1)
                v.tensor_scalar(stat[:, u % 2, 0, :], stat[:, u % 2, 0, :], -QSCALE, None,
                                ALU.mult).then_inc(max_ready, 1)

            def normalise(st, u):
                dve.wait_ge(exp_ready, st.unit(u) + 1)
                v.reciprocal(stat[:, u % 2, 2, :], stat[:, u % 2, 1, :]).then_inc(inv_step, 1)
                dve.wait_ge(inv_step, st.unit(u) + 1)
                v.tensor_tensor(prob[:, u % 2], prob[:, u % 2],
                                stat[:, u % 2, 2, :].unsqueeze(2).broadcast_to([P, GQ, SEQ]),
                                ALU.mult).then_inc(prob_ready, 1)

            def probs_lo(st, u):
                dve.wait_ge(pt_hi, st.unit(u) + 1)
                v.tensor_tensor(ptl[:, u % 2, :], turn_ps[:], pth[:, u % 2, :].bitcast(F32),
                                ALU.subtract).then_inc(turn_free, 1)

            def attn_lo(st, u):
                dve.wait_ge(o_hi, st.unit(u) + 1)
                tok = slice(u * SEQ, (u + 1) * SEQ)
                v.tensor_tensor(ol[:, :, tok], attn_ps[:].rearrange("p (h s) -> p h s", h=GQ),
                                oh[:, :, tok].bitcast(F32), ALU.subtract).then_inc(attn_free, 1)

            def add_chunk(st, o):
                dve.wait_ge(chunk_ready, st.chunk(6 + o) + 1)
                v.tensor_tensor(acc[:, o, :], acc[:, o, :], chunk_ps[st.bank(6 + o)][:], ALU.add).then_inc(chunk_free, 1)

            def step(st, nxt):
                maxima(st, 0)
                weights(*nxt(3))
                normalise(st, 0)
                rope(st, 0, 0)
                probs_lo(st, 0)
                maxima(st, 1)
                normalise(st, 1)
                weights(*nxt(4))
                rope_lo(st, 0, 0)
                probs_lo(st, 1)
                attn_lo(st, 0)
                maxima(st, 2)
                v_copy(st)
                normalise(st, 2)
                weights(*nxt(5))
                rope(st, 2, 1)
                probs_lo(st, 2)
                attn_lo(st, 1)
                maxima(st, 3)
                normalise(st, 3)
                weights(*nxt(6))
                rope_lo(st, 2, 1)
                rope(st, 3, 2)
                probs_lo(st, 3)
                attn_lo(st, 2)
                weights(*nxt(7))
                rope_lo(st, 3, 2)
                rope(st, 4, 3)
                attn_lo(st, 3)
                weights(*nxt(8))
                rope_lo(st, 4, 3)
                v_split(st)
                rope(st, 5, 4)
                weights(*nxt(9))
                rope_lo(st, 5, 4)
                for o in range(A8):
                    add_chunk(st, o)
                    if o % 2 == 1 and o < 7:
                        weights(*nxt(10 + o // 2))

            for given, count in ((w_lo, NSLOT), (chunk_free, NSLOT), (turn_free, 1), (score_free, 2), (attn_free, 1)):
                dve.sem_inc(given, count)
            dve.wait_ge(in_const, 16 * 6)
            with dve.Fori(0, TT) as tt:
                first, last = First(tt), Last(tt)
                for j in range(3):
                    weights(first, j)
                layer_norm(tt, 0)
                s1 = Step(tt, 0, 0)
                for j in range(6):
                    weights(*((first, j + 3) if j < 3 else (s1, j - 3)))
                    if j == 2:
                        v_copy(first)
                    elif j >= 1:
                        m = (0, None, 1, 2, 3, 4)[j - 1]
                        rope(first, j - 1, m)
                        rope_lo(first, j - 1, m)
                rope(first, 5, 4)
                v_split(first)
                rope_lo(first, 5, 4)
                with dve.Fori(0, 3) as it:
                    for q in range(2):
                        st = Step(tt, it, q)
                        step(st, lambda j: (st, j))
                st = Step(tt, 3, 0)
                step(st, lambda j: (st, j) if j < 10 else (last, j - 4))
                maxima(last, 0)
                normalise(last, 0)
                probs_lo(last, 0)
                maxima(last, 1)
                normalise(last, 1)
                probs_lo(last, 1)
                attn_lo(last, 0)
                maxima(last, 2)
                normalise(last, 2)
                probs_lo(last, 2)
                attn_lo(last, 1)
                maxima(last, 3)
                normalise(last, 3)
                probs_lo(last, 3)
                attn_lo(last, 2)
                attn_lo(last, 3)
                for o in range(A8):
                    if o % 2 == 0:
                        weights(last, 9 + o // 2)
                    add_chunk(last, o)
                layer_norm(tt, 1)
                for o in range(A8):
                    if o < 5:
                        weights(last, 13 + o)
                    dve.wait_ge(chunk_ready, last.chunk(14 + o) + 1)
                    v.scalar_tensor_tensor(acc[:, o, :], chunk_ps[last.bank(14 + o)][:], bias[:, o:o + 1],
                                           acc[:, o, :], ALU.add, ALU.add).then_inc(chunk_free, 1)


def program(nc, ins, out_dram, h_dram, weff_dram):
    s4d_and_lora_fold(nc, ins, h_dram, weff_dram)
    transformer(nc, ins, h_dram, weff_dram, out_dram)


def constants():
    f = np.float32
    tab = np.concatenate([np.arange(B0), B0 * np.arange(B1), P * np.arange(A8)]).astype(f)
    inv_freq = f(1.0) / f(10000.0) ** (np.arange(0, HD, 2, dtype=f) / f(HD))
    freqs = np.arange(SEQ, dtype=f)[:, None] * inv_freq[None, :]
    emb = np.concatenate([freqs, freqs], axis=-1)
    cos, sin = np.cos(emb).astype(f).T, np.sin(emb).astype(f).T
    sign = np.where(np.arange(HD) < HD // 2, f(-1), f(1))[:, None]
    pos = np.arange(SEQ)
    return {
        "tab": np.broadcast_to(tab, (P, NTAB)).copy(),
        "cos": cos.copy(), "sin": (sin * sign).astype(f),
        "mask": np.where(pos[:, None] >= pos[None, :], f(0), np.finfo(f).min).astype(f),
        "ident": np.eye(P, dtype=f),
        "mean_w": np.full((P, P), 1.0 / D, f),
    }


def kernel(x, L0_tok_log_dt, L0_tok_B, L0_tok_inv_A_real, L0_tok_A_imag, L0_attn_wq, L0_attn_wk, L0_attn_wv,
           L0_attn_wo, L0_ffn_W, L0_ffn_bias, L0_ffn_A, L0_ffn_Bf, L0_ffn_coeffs, L0_ffn_scales):
    import concourse.bacc as bacc
    from concourse.bass_utils import run_bass_kernel_spmd

    def both(y):
        return np.concatenate([np.asarray(y).T] * 2, axis=0)

    c = np.asarray(x).transpose(3, 2, 1, 0)
    b = np.asarray(L0_tok_B)
    wq = np.asarray(L0_attn_wq).reshape(NKV, GQ, HD, A8, P)
    wk = np.asarray(L0_attn_wk).reshape(NKV, 1, HD, A8, P)
    wv = np.asarray(L0_attn_wv).reshape(NKV, 1, HD, A8, P)
    wqkv = np.concatenate([wk, wv, wq], axis=1).transpose(0, 1, 4, 3, 2).reshape(NKV, 6, P, D)
    wo = np.asarray(L0_attn_wo).reshape(4, 256, NKV, GQ, HD).transpose(2, 0, 4, 3, 1).reshape(NKV, 4, P, D)
    per_expert = [np.repeat(np.asarray(y), ER // 16).reshape(2, P).T for y in (L0_ffn_coeffs, L0_ffn_scales)]
    arrays = {
        "small": np.stack([np.broadcast_to(np.asarray(L0_tok_log_dt), (P, SEQ)), both(L0_tok_inv_A_real),
                           both(L0_tok_A_imag), both(b[..., 0]), both(b[..., 1])], axis=1),
        "coef": np.concatenate([c.transpose(1, 0, 2, 3)] * 2, axis=0),
        "lora_a": np.asarray(L0_ffn_A).reshape(2, P, D).transpose(1, 0, 2),
        "lora_b": np.asarray(L0_ffn_Bf).transpose(0, 2, 1).reshape(2, P, D).transpose(1, 0, 2),
        "lora_w": np.concatenate(per_expert, axis=1),
        "wt": np.asarray(L0_ffn_W).T.reshape(A8, P, D),
        "wqkv": wqkv, "wo": wo,
        "bias": np.asarray(L0_ffn_bias).reshape(A8, P).T,
    }
    arrays.update(constants())
    arrays = {k: np.ascontiguousarray(v) for k, v in arrays.items()}

    nc = bacc.Bacc("TRN2", target_bir_lowering=False, num_devices=1)
    ins = {k: nc.dram_tensor(f"in_{k}", v.shape, mybir.dt.from_np(v.dtype), kind="ExternalInput").ap()
           for k, v in arrays.items()}
    out = nc.dram_tensor("out_t", (TT, A8, P, NT), F32, kind="ExternalOutput").ap()
    h_dram = nc.dram_tensor("h_t", (TT, P, A8, CPT, SEQ), F32, kind="Internal").ap()
    weff = nc.dram_tensor("weff", (A8, P, A8, P), F32, kind="Internal").ap()
    program(nc, ins, out, h_dram, weff)
    r = run_bass_kernel_spmd(nc, [{f"in_{k}": v for k, v in arrays.items()}], core_ids=[0])
    y = r.results[0]["out_t"].reshape(TT, D, CPT, SEQ)
    return y.transpose(0, 2, 3, 1).reshape(NB, SEQ, D)
```

```python
import math
from contextlib import ExitStack

import numpy as np

import concourse.bass as bass
from concourse import mybir

F32 = mybir.dt.float32
F32R = mybir.dt.float32r
I32 = mybir.dt.int32
ALU = mybir.AluOpType
ACT = mybir.ActivationFunctionType

NB, SEQ, NS = 16, 128, 64
D = 1024
A8, P = D // 128, 128
HD, NKV, GQ = 128, 8, 4
TT = 4
NT = NB * SEQ // TT
CPT = NT // SEQ
QSCALE = 1.0 / math.sqrt(HD)
EPS = 1e-5
ER = 256

NRAW, NSPLIT = 2, 4
NCHUNK, NRES = 4, 4
U_ALL = TT * NKV * CPT
H_STORES = 2 * (TT - 1)

B0, B1 = 16, 8
NTAB = B0 + B1 + A8
HBLK = 8
DVE_POS = 4
MAGIC = 12582912.0
TWO_PI_LOW = 6.283185


def s4d_and_lora_fold(nc, ins, kept, h_dram, weff_dram):
    acc, h_stored, ident = kept.acc, kept.h_stored, kept.ident
    ctx = ExitStack()
    with ctx:
        def sb(name, shape, dt=F32):
            return ctx.enter_context(nc.sbuf_tensor(name, shape, dt))

        def sem(name):
            return ctx.enter_context(nc.semaphore(name))

        hbuf = sb("hbuf", [P, TT - 1, A8, NT])
        small = sb("small", [P, 5, SEQ])
        tab = sb("tab", [P, NTAB])
        coef = sb("coef", [P, 2, SEQ, NB])
        flat = hbuf[:].rearrange("p t a n -> p (t a n)")

        def big(i):
            return flat[:, i * SEQ * NTAB:(i + 1) * SEQ * NTAB].rearrange("p (s j) -> p s j", j=NTAB)

        turn, absturn, mag = big(0), big(1), big(2)
        cosr = sb("cosr", [P, SEQ, NTAB])
        sini = sb("sini", [P, SEQ, NTAB])
        x0 = sb("x0", [P, SEQ, B0])
        y0 = sb("y0", [P, SEQ, B0])
        wa = sb("wa", [P, SEQ, A8])
        wb = sb("wb", [P, SEQ, A8])
        w2a = sb("w2a", [P, 2, HBLK, P])
        w2b = sb("w2b", [P, 2, HBLK, P])
        pa = sb("pa", [P, 2, HBLK, P])
        pb = sb("pb", [P, 2, HBLK, P])
        ex = sb("ex", [P, 2, SEQ])
        t = sb("t", [P, 8, SEQ])
        ti = sb("ti", [P, 2, SEQ], I32)
        half_pi = sb("half_pi", [P, 1])
        lora_a = sb("lora_a", [P, 2, D])
        lora_b = sb("lora_b", [P, 2, D])
        lora_w = sb("lora_w", [P, 4])
        lora_wt = kept.raw[:, 0, :].rearrange("p (n o) -> p n o", n=2)
        lora_out = kept.raw[:, 1, :].rearrange("p (n o) -> p n o", n=2)
        banks = [ctx.enter_context(nc.psum_tensor(f"s4d{i}", [P, 512], F32)) for i in range(8)]

        in_small, in_coef = sem("in_small"), sem("in_coef")
        in_lora = sem("in_lora")
        in_wt = [sem(f"in_wt{i}") for i in range(2)]
        dve_done = sem("dve_done")
        act_done = sem("act_done")
        lora_b_ready = sem("lora_b_ready")
        lora_ready, lora_read = sem("lora_ready"), sem("lora_read")
        lora_stored = [sem(f"lora_stored{i}") for i in range(2)]
        table_part = sem("table_part")
        w2_mul, blk_ready, blk_used, h_read = sem("w2_mul"), sem("blk_ready"), sem("blk_used"), sem("h_read")
        pool_ready = sem("pool_ready")
        NBLK = SEQ // HBLK
        marks = {}
        block = ctx.enter_context(nc.Block())

        tabs = tab[:].unsqueeze(1).broadcast_to([P, SEQ, NTAB])

        def rows(x):
            return x.unsqueeze(2).broadcast_to([P, SEQ, NTAB])

        def product(engine, n, dst, outer, inner, first, last):
            rows_o, rows_i = outer.shape[-1], inner.shape[-1]
            pos = slice(n * HBLK + first, n * HBLK + last)
            shape = [P, last - first, rows_o, rows_i]
            return engine.tensor_tensor(
                dst[:, n % 2, first:last].rearrange("p s (o i) -> p s o i", o=rows_o),
                outer[:, pos].unsqueeze(3).broadcast_to(shape),
                inner[:, pos].unsqueeze(2).broadcast_to(shape), ALU.mult)

        @block.sync
        def _(sp):
            sp.dma_start(small[:], ins["small"]).then_inc(in_small, 16)
            sp.dma_start(tab[:], ins["tab"]).then_inc(in_small, 16)
            sp.dma_start(lora_w[:], ins["lora_w"]).then_inc(in_lora, 16)
            sp.dma_start(ident[:], ins["ident"]).then_inc(in_lora, 16)
            sp.dma_start(lora_b[:], ins["lora_b"]).then_inc(in_lora, 16)
            sp.dma_start(lora_a[:], ins["lora_a"]).then_inc(in_lora, 16)

            def load_wt(n):
                a, oh = n // 2, n % 2
                sp.dma_start(lora_wt[:, n % 2, :], ins["wt"][a, :, oh * 512:(oh + 1) * 512]).then_inc(in_wt[n % 2], 16)

            load_wt(0)
            load_wt(1)
            sp.dma_start(coef[:], ins["coef"]).then_inc(in_coef, 16)
            for name, dst in (("cos", kept.cos), ("sin", kept.sin), ("mask", kept.mask),
                              ("mean_w", kept.mean_w), ("bias", kept.bias)):
                sp.dma_start(dst[:], ins[name]).then_inc(kept.in_const, 16)
            for n in range(16):
                a, oh = n // 2, n % 2
                if n + 1 < 16 and n >= 1:
                    sp.wait_ge(lora_ready, n)
                    load_wt(n + 1)
                sp.wait_ge(lora_read, n + 1)
                sp.dma_start(weff_dram[oh * 4:oh * 4 + 4, :, a, :].rearrange("t p o -> p t o"),
                             lora_out[:, n % 2, :].rearrange("p (t o) -> p t o", t=4)).then_inc(lora_stored[n % 2], 16)
            for i in range(2):
                sp.wait_ge(lora_stored[i], 16 * 8)
            for j in range(NRAW):
                sp.dma_start(kept.raw[:, j, :], ins["wqkv"][0, j]).then_inc(kept.raw_in[j], 16)
            for half in range(2):
                s = slice(half * SEQ // 2, (half + 1) * SEQ // 2)
                sp.wait_ge(h_read, (half + 1) * SEQ // 8)
                for tile in range(1, TT):
                    sp.dma_start(h_dram[tile].rearrange("p a (c s) -> p (a c) s", c=CPT)[:, :, s],
                                 hbuf[:, tile - 1].rearrange("p a (c s) -> p (a c) s", c=CPT)[:, :, s]).then_inc(h_stored, 16)

        @block.vector
        def _(dve):
            n_done = [0]

            def link(ins_):
                n_done[0] += 1
                ins_.then_inc(dve_done, 1)
                dve.wait_ge(dve_done, n_done[0])

            v = nc.vector
            link(v.memset(half_pi[:], math.pi / 2))
            dve.wait_ge(in_small, 32)
            arg = small[:, 0:2, :]
            k2, r2, e2 = t[:, 0:2, :], t[:, 2:4, :], t[:, 4:6, :]
            link(v.tensor_scalar(k2, arg, 1.4426950408889634, MAGIC, ALU.mult, ALU.add))
            link(v.tensor_scalar(k2, k2, MAGIC, -126.0, ALU.subtract, ALU.max))
            link(v.tensor_scalar(k2, k2, 127.0, None, ALU.min))
            link(v.scalar_tensor_tensor(r2, k2, -0.693359375, arg, ALU.mult, ALU.add))
            link(v.scalar_tensor_tensor(r2, k2, 2.12194440e-4, r2, ALU.mult, ALU.add))
            link(v.tensor_scalar(ti[:], k2, 127.0, 8388608.0, ALU.add, ALU.mult))
            link(v.tensor_scalar(e2, r2, 1.0 / 5040, 1.0 / 720, ALU.mult, ALU.add))
            for c in (1.0 / 120, 1.0 / 24, 1.0 / 6, 0.5, 1.0):
                link(v.tensor_tensor(e2, e2, r2, ALU.mult))
                link(v.tensor_scalar(e2, e2, c, None, ALU.add))
            link(v.tensor_tensor(e2, e2, r2, ALU.mult))
            link(v.tensor_scalar(e2, e2, 1.0, None, ALU.add))
            link(v.tensor_tensor(ex[:], e2, ti[:].bitcast(F32), ALU.mult))
            dt, are = ex[:, 0, :], ex[:, 1, :]
            ar, theta, vturn, kk = t[:, 0, :], t[:, 1, :], t[:, 2, :], t[:, 3, :]
            link(v.scalar_tensor_tensor(ar, are, -1.0, dt, ALU.mult, ALU.mult))
            marks["decay"] = n_done[0]
            link(v.tensor_tensor(theta, small[:, 2, :], dt, ALU.mult))
            link(v.tensor_scalar(kk, theta, 1.0 / (2 * math.pi), MAGIC, ALU.mult, ALU.add))
            link(v.tensor_scalar(kk, kk, MAGIC, None, ALU.subtract))
            link(v.scalar_tensor_tensor(vturn, kk, -6.28125, theta, ALU.mult, ALU.add))
            link(v.scalar_tensor_tensor(vturn, kk, -0.0019353071795864769, vturn, ALU.mult, ALU.add))
            link(v.tensor_scalar(vturn, vturn, 1.0 / (2 * math.pi), None, ALU.mult))

            dve.wait_ge(in_lora, 64)
            link(v.tensor_tensor(lora_w[:, 0:2], lora_w[:, 0:2], lora_w[:, 2:4], ALU.mult))
            for k in range(2):
                ins_ = v.tensor_scalar(lora_b[:, k, :], lora_b[:, k, :], lora_w[:, k:k + 1], None, ALU.mult)
                ins_.then_inc(lora_b_ready, 1)
            link(v.tensor_tensor(turn, rows(vturn), tabs, ALU.mult))
            link(v.tensor_scalar(absturn, turn, MAGIC, None, ALU.add))
            link(v.scalar_tensor_tensor(turn, absturn, MAGIC, turn, ALU.subtract, ALU.subtract))
            marks["turn"] = n_done[0]
            link(v.scalar_tensor_tensor(absturn, turn, -1.0, turn, ALU.mult, ALU.max))
            marks["abs"] = n_done[0]
            em, lim, mask = t[:, 4, :], t[:, 5, :], ti[:, 0, :]
            link(v.tensor_scalar(lim, ar, -0.5, None, ALU.max))
            link(v.tensor_scalar(em, lim, 1.0 / 40320, 1.0 / 5040, ALU.mult, ALU.add))
            for c in (1.0 / 720, 1.0 / 120, 1.0 / 24, 1.0 / 6, 0.5, 1.0):
                link(v.tensor_tensor(em, em, lim, ALU.mult))
                link(v.tensor_scalar(em, em, c, None, ALU.add))
            link(v.tensor_tensor(em, em, lim, ALU.mult))
            link(v.tensor_scalar(mask, ar, -0.5, None, ALU.is_lt))
            dve.wait_ge(act_done, 4)
            link(v.tensor_scalar(lim, mag[:, :, 1], -1.0, None, ALU.add))
            link(v.copy_predicated(em, mask, lim))
            s1, c1, sh = sini[:, :, 1], cosr[:, :, 1], t[:, 3, :]
            c1m, er, ei = t[:, 5, :], t[:, 6, :], t[:, 7, :]
            link(v.scalar_tensor_tensor(c1m, sh, -2.0, sh, ALU.mult, ALU.mult))
            link(v.tensor_tensor(er, em, c1, ALU.mult))
            link(v.tensor_tensor(er, er, c1m, ALU.add))
            link(v.scalar_tensor_tensor(ei, em, 1.0, s1, ALU.add, ALU.mult))
            aim, den, tmp = small[:, 2, :], t[:, 0, :], t[:, 1, :]
            link(v.tensor_tensor(den, are, are, ALU.mult))
            link(v.tensor_tensor(tmp, aim, aim, ALU.mult))
            link(v.tensor_tensor(den, den, tmp, ALU.add))
            link(v.reciprocal(den, den))
            link(v.tensor_scalar(den, den, 2.0, None, ALU.mult))
            xq, yq = t[:, 2, :], t[:, 3, :]
            link(v.tensor_tensor(xq, ei, aim, ALU.mult))
            link(v.tensor_tensor(tmp, er, are, ALU.mult))
            link(v.tensor_tensor(xq, xq, tmp, ALU.subtract))
            link(v.tensor_tensor(xq, xq, den, ALU.mult))
            link(v.tensor_tensor(yq, ei, are, ALU.mult))
            link(v.tensor_tensor(tmp, er, aim, ALU.mult))
            link(v.tensor_tensor(yq, yq, tmp, ALU.add))
            link(v.scalar_tensor_tensor(yq, yq, -1.0, den, ALU.mult, ALU.mult))
            gr, gi = t[:, 4, :], t[:, 5, :]
            br, bi = small[:, 3, :], small[:, 4, :]
            link(v.tensor_tensor(gr, xq, br, ALU.mult))
            link(v.tensor_tensor(tmp, yq, bi, ALU.mult))
            link(v.tensor_tensor(gr, gr, tmp, ALU.subtract))
            link(v.tensor_tensor(gi, xq, bi, ALU.mult))
            link(v.tensor_tensor(tmp, yq, br, ALU.mult))
            link(v.tensor_tensor(gi, gi, tmp, ALU.add))
            rest = slice(B0, NTAB)
            link(v.tensor_tensor(cosr[:, :, rest], cosr[:, :, rest], mag[:, :, rest], ALU.mult))
            link(v.tensor_tensor(sini[:, :, rest], sini[:, :, rest], mag[:, :, rest], ALU.mult))

            def eight(x):
                return x.unsqueeze(2).broadcast_to([P, SEQ, A8])

            rot, iot = cosr[:, :, B0 + B1:NTAB], sini[:, :, B0 + B1:NTAB]

            def scratch(x):
                return x[:, 0].rearrange("p s q -> p (s q)").rearrange("p (s a) -> p s a", a=A8)

            grr, gii, tm = scratch(pa), scratch(pb), scratch(w2a)
            link(v.tensor_tensor(grr, rot, eight(gr), ALU.mult))
            link(v.tensor_tensor(tm, iot, eight(gi), ALU.mult))
            link(v.tensor_tensor(grr, grr, tm, ALU.subtract))
            link(v.tensor_tensor(gii, rot, eight(gi), ALU.mult))
            link(v.tensor_tensor(tm, iot, eight(gr), ALU.mult))
            link(v.tensor_tensor(gii, gii, tm, ALU.add))
            hr, hi = slice(0, 64), slice(64, 128)
            link(v.tensor_copy(wa[hr], grr[hr]))
            link(v.tensor_scalar(wa[hi], gii[hi], -1.0, None, ALU.mult))
            link(v.tensor_scalar(wb[hr], gii[hr], -1.0, None, ALU.mult))
            link(v.tensor_scalar(wb[hi], grr[hi], -1.0, None, ALU.mult))
            marks["weights"] = n_done[0]
            dve.wait_ge(in_coef, 16)
            dve.wait_ge(table_part, 5)
            dve.wait_ge(act_done, 5)

            for n in range(NBLK):
                d = n % 2
                if n >= 2:
                    dve.wait_ge(blk_used, n - 1)
                product(v, n, w2a, cosr[:, :, B0:B0 + B1], x0, 0, HBLK)
                product(v, n, w2b, sini[:, :, B0:B0 + B1], y0, 0, HBLK).then_inc(w2_mul, 1)
                product(v, n, pa, coef[:, 0], wa, 0, DVE_POS)
                dve.wait_ge(w2_mul, n + 1)
                v.tensor_tensor(w2a[:, d], w2a[:, d], w2b[:, d], ALU.add).then_inc(blk_ready, 1)

        @block.gpsimd
        def _(pool):
            g = nc.gpsimd
            pool.wait_ge(in_small, 32)
            pool.wait_ge(dve_done, marks["decay"])
            g.tensor_tensor(mag, rows(t[:, 0, :]), tabs, ALU.mult).then_inc(table_part, 1)
            pool.wait_ge(act_done, 3)
            lower, upper = slice(0, 64), slice(64, 128)
            for i, (dst, part, table) in enumerate(((y0, lower, sini), (x0, lower, cosr),
                                                    (x0, upper, sini), (y0, upper, cosr))):
                pool.wait_ge(table_part, i + 1)
                g.tensor_tensor(dst[part], table[part, :, 0:B0], mag[part, :, 0:B0], ALU.mult).then_inc(table_part, 1)
            pool.wait_ge(in_coef, 16)
            pool.wait_ge(dve_done, marks["weights"])
            pool.wait_ge(table_part, 5)
            for n in range(NBLK):
                if n >= 2:
                    pool.wait_ge(blk_used, n - 1)
                product(g, n, pb, coef[:, 1], wb, 0, HBLK)
                product(g, n, pa, coef[:, 0], wa, DVE_POS, HBLK).then_inc(pool_ready, 1)

        @block.scalar
        def _(act):
            def lora_copies(some):
                for n in some:
                    act.wait_ge(lora_ready, n + 1)
                    if n >= 2:
                        act.wait_ge(lora_stored[n % 2], 16 * (n // 2))
                    nc.scalar.activation(lora_out[:, n % 2, :], banks[n % 2][:], ACT.Copy).then_inc(lora_read, 1)

            act.wait_ge(table_part, 1)
            nc.scalar.activation(mag, mag, ACT.Exp).then_inc(act_done, 1)
            lora_copies(range(0, 1))
            act.wait_ge(dve_done, marks["turn"])
            nc.scalar.activation(sini[:], turn, ACT.Sin, scale=-TWO_PI_LOW).then_inc(act_done, 1)
            lora_copies(range(1, 2))
            act.wait_ge(dve_done, marks["abs"])
            nc.scalar.activation(cosr[:], absturn, ACT.Sin, bias=half_pi[:], scale=-TWO_PI_LOW).then_inc(act_done, 1)
            nc.scalar.activation(t[:, 3, :], turn[:, :, 1], ACT.Sin, scale=TWO_PI_LOW / 2).then_inc(act_done, 1)
            lora_copies(range(2, 6))
            act.wait_ge(table_part, 2)
            nc.scalar.activation(y0[0:64], y0[0:64], ACT.Copy, scale=-1.0).then_inc(act_done, 1)
            lora_copies(range(6, 16))
            for n in range(SEQ // 4):
                act.wait_ge(blk_used, n // 2 + 1)
                s = slice(4 * n, 4 * n + 4)
                got = banks[2 + n % 6][:].rearrange("p (s c a) -> p s c a", s=4, a=A8)
                for tile in range(TT):
                    dst = (hbuf[:, tile - 1] if tile else acc[:]).rearrange("p a (c s) -> p s c a", c=CPT)
                    last = nc.scalar.activation(dst[:, s], got[:, :, tile * CPT:(tile + 1) * CPT], ACT.Copy)
                last.then_inc(h_read, 1)

        @block.tensor
        def _(pe):
            pe.wait_ge(in_lora, 64)
            pe.wait_ge(lora_b_ready, 2)
            for n in range(16):
                a, oh = n // 2, n % 2
                if n >= 2:
                    pe.wait_ge(lora_read, n - 1)
                for k in range(2):
                    nc.tensor.matmul(banks[n % 2][:], lora_a[:, k, a * P:(a + 1) * P],
                                     lora_b[:, k, oh * 512:(oh + 1) * 512], start=(k == 0), stop=False)
                pe.wait_ge(in_wt[n % 2], 16 * (n // 2 + 1))
                nc.tensor.matmul(banks[n % 2][:], ident[:], lora_wt[:, n % 2, :],
                                 start=False, stop=True).then_inc(lora_ready, 1)
            for n in range(NBLK):
                pe.wait_ge(blk_ready, n + 1)
                pe.wait_ge(pool_ready, n + 1)
                for half in range(2):
                    m = 2 * n + half
                    if m >= 6:
                        pe.wait_ge(h_read, m - 5)
                    for j in range(4):
                        s = half * 4 + j
                        out = banks[2 + m % 6][:, j * P:(j + 1) * P]
                        nc.tensor.matmul(out, w2a[:, n % 2, s, :], pa[:, n % 2, s, :], start=True, stop=False)
                        last = nc.tensor.matmul(out, w2a[:, n % 2, s, :], pb[:, n % 2, s, :], start=False, stop=True)
                last.then_inc(blk_used, 1)


class Step:

    def __init__(self, tile, it, q):
        self.tile_no, self.it, self.q = tile, it, q
        self.new, self.old = 1 - q, q

    def at(self, each, rest):
        value = each * (1 + self.q) + rest
        for factor, variable in ((8 * each, self.tile_no), (2 * each, self.it)):
            value = variable * factor + value
        return value

    def tile(self, j):
        return self.at(10, j - 4)

    def split_slot(self, j):
        return (10 * (1 + self.q) - 4 + j) % NSPLIT

    def raw_slot(self, j):
        return j % NRAW

    def raw_uses(self, j):
        return self.at(10 // NRAW, (j - 4) // NRAW + 1)

    def slot_free(self, j):
        return self.chunk(j - 3 if j < 10 else 8 + 2 * (j - 10) if j < 14 else j + 1)

    def chunk(self, m):
        return self.at(14, m - 8)

    def bank(self, m):
        return (14 * (1 + self.q) - 8 + m) % NCHUNK

    def unit(self, u):
        return self.at(4, u - 4)

    def heads(self):
        return self.at(1, 0)


class First(Step):

    def __init__(self):
        self.new = 0

    def tile(self, j):
        return j

    def split_slot(self, j):
        return j % NSPLIT

    def raw_uses(self, j):
        return j // NRAW + 1

    def slot_free(self, j):
        return j - 3

    def chunk(self, m):
        return m

    def bank(self, m):
        return m % NCHUNK

    def heads(self):
        return 0


LAST = Step(TT - 1, 3, 1)
LAST7 = Step(TT - 1, 3, 0)


def ffn_chunk(c):
    return (c, c) if c < 6 else (c + 8, c + 4)


def transformer(nc, ins, kept, h_dram, weff_dram, out_dram):
    acc, raw, h_stored, in_const, raw_in = kept.acc, kept.raw, kept.h_stored, kept.in_const, kept.raw_in
    cos, sin, mask, ident, mean_w, bias = kept.cos, kept.sin, kept.mask, kept.ident, kept.mean_w, kept.bias
    ctx = ExitStack()
    with ctx:
        def sb(name, shape, dt=F32):
            return ctx.enter_context(nc.sbuf_tensor(name, shape, dt))

        def sem(name):
            return ctx.enter_context(nc.semaphore(name))

        qh, ql = sb("qh", [P, 2, GQ, NT], F32R), sb("ql", [P, 2, GQ, NT], F32R)
        kh, kl = sb("kh", [P, 2, NT], F32R), sb("kl", [P, 2, NT], F32R)
        vh, vl = sb("vh", [P, 2, NT], F32R), sb("vl", [P, 2, NT], F32R)
        dev = sb("dev", [P, A8, NT])
        sq = sb("sq", [P, 2, NT])
        total, total_sq = sb("total", [P, NT]), sb("total_sq", [P, NT])
        mean = sb("mean", [P, NT])
        rstd = sb("rstd", [P, NT])
        xh, xl = sb("xh", [P, A8, NT], F32R), sb("xl", [P, A8, NT], F32R)
        wh, wl = sb("wh", [P, NSPLIT, D], F32R), sb("wl", [P, NSPLIT, D], F32R)
        vt = sb("vt", [P, NT])
        rot, direct, roped = sb("rot", [P, NT]), sb("direct", [P, NT]), sb("roped", [P, NT])
        prob = sb("prob", [P, 2, GQ, SEQ])
        stat = sb("stat", [P, 2, 3, GQ])
        pth, ptl = sb("pth", [P, NT], F32R), sb("ptl", [P, NT], F32R)
        oh, ol = sb("oh", [P, GQ, NT], F32R), sb("ol", [P, GQ, NT], F32R)
        res = sb("res", [P, NRES, NT])

        chunk_ps = [ctx.enter_context(nc.psum_tensor(f"chunk{i}", [P, NT], F32)) for i in range(NCHUNK)]
        score_ps = [ctx.enter_context(nc.psum_tensor(f"score{i}", [P, NT], F32)) for i in range(2)]
        turn_ps = ctx.enter_context(nc.psum_tensor("turn", [P, NT], F32))
        attn_ps = ctx.enter_context(nc.psum_tensor("attn", [P, NT], F32))

        w_hi = sem("w_hi")
        w_lo = sem("w_lo")
        chunk_ready, chunk_free = sem("chunk_ready"), sem("chunk_free")
        rot_ready, rope_step, rope_ready = sem("rot_ready"), sem("rope_step"), sem("rope_ready")
        r_hi, r_lo = sem("r_hi"), sem("r_lo")
        turn_ready, turn_free = sem("turn_ready"), sem("turn_free")
        v_hi = sem("v_hi")
        score_ready, score_free = sem("score_ready"), sem("score_free")
        max_step, max_ready, exp_ready = sem("max_step"), sem("max_ready"), sem("exp_ready")
        inv_step, prob_ready = sem("inv_step"), sem("prob_ready")
        pt_hi = sem("pt_hi")
        attn_ready, attn_free = sem("attn_ready"), sem("attn_free")
        o_hi = sem("o_hi")
        dev_in = sem("dev_in")
        acc_in = sem("acc_in")
        acc_tiles = sem("acc_tiles")
        h2_half = sem("h2_half")
        sum_step, total_ready = sem("sum_step"), sem("total_ready")
        mean_ready, mean_read = sem("mean_ready"), sem("mean_read")
        dev_ready, sq_ready, sq_read = sem("dev_ready"), sem("sq_ready"), sem("sq_read")
        var_step, var_ready, rstd_step, std_ready = sem("var_step"), sem("var_ready"), sem("rstd_step"), sem("std_ready")
        norm_ready, x_hi, x_lo = sem("norm_ready"), sem("x_hi"), sem("x_lo")
        res_in = [sem(f"res_in{i}") for i in range(NRES)]
        res_out = [sem(f"res_out{i}") for i in range(NRES)]

        q_as_x = [t_[:].rearrange("p z h s -> p (z h) s") for t_ in (qh, ql)]

        def x_of(job):
            return q_as_x if job in (5, 7) else (xh[:], xl[:])

        block = ctx.enter_context(nc.Block())

        @block.sync
        def _(sp):
            def load(st, j, src):
                sp.wait_ge(w_lo, st.tile(j) + 1)
                sp.dma_start(raw[:, j % NRAW, :], src).then_inc(raw_in[j % NRAW], 16)

            def step_loads(st, new, old):
                for j in range(6):
                    load(st, j, ins["wqkv"][new, j])
                for j in range(4):
                    load(st, 6 + j, ins["wo"][old, j])

            def tile_loads(tile):
                with sp.Fori(0, 3) as it:
                    for q in range(2):
                        step_loads(Step(tile, it, q), it * 2 + (1 + q), it * 2 + q)
                step_loads(Step(tile, 3, 0), 7, 6)

            for j in range(NRAW, 6):
                load(First(), j, ins["wqkv"][0, j])
            with sp.Fori(0, TT - 1) as tile:
                tile_loads(tile)
                step_loads(Step(tile, 3, 1), 0, 7)
            tile_loads(TT - 1)

            def tile_of(slot):
                if 6 <= slot < 10:
                    return ins["wo"][NKV - 1, slot - 6]
                c = slot if slot < 6 else slot - 4
                return weff_dram[c % A8].rearrange("p a o -> p (a o)")

            def residual(c):
                t_, o, slot = c // A8, c % A8, c % NRES
                if c >= NRES:
                    sp.wait_ge(res_out[slot], 16 * (c // NRES))
                if c % A8 == 0:
                    sp.wait_ge(h2_half, 32 * (t_ + 1))
                sp.dma_start(res[:, slot, :], h_dram[t_][:, o, :]).then_inc(res_in[slot], 16)

            def store(c):
                slot = c % NRES
                sp.wait_ge(chunk_free, LAST.chunk(ffn_chunk(c)[0]) + (NCHUNK + 1))
                sp.dma_start(out_dram[c // A8, c % A8], res[:, slot, :]).then_inc(res_out[slot], 16)

            slots = 10 + TT * A8 - 6
            for j in range(5):
                load(LAST, j, tile_of(j))
            for slot in range(slots + 1):
                if slot + 5 < slots:
                    load(LAST, slot + 5, tile_of(slot + 5))
                if slot < 6 or 10 <= slot < slots:
                    residual(slot if slot < 6 else slot - 4)
                if 1 <= slot < 7 or 10 < slot:
                    store(slot - 1 if slot < 7 else slot - 5)
            for slot in range(NRES):
                sp.wait_ge(res_out[slot], 16 * (TT * A8 // NRES))

        @block.gpsimd
        def _(pool):
            g = nc.gpsimd

            def job(n, dst):
                pool.wait_ge(dev_in, n * 16)
                for a in range(1, A8):
                    if a > 1:
                        pool.wait_ge(sum_step, n * 6 + (a - 7))
                    ins_ = g.tensor_tensor(total[:], dst[:, 0, :] if a == 1 else total[:], dst[:, a, :], ALU.add)
                    ins_.then_inc(total_ready if a == A8 - 1 else sum_step, 1)
                pool.wait_ge(mean_read, n * 1)
                for a in range(A8):
                    g.tensor_tensor(dst[:, a, :], dst[:, a, :], mean[:], ALU.subtract).then_inc(dev_ready, 1)
                for a in range(1, A8):
                    pool.wait_ge(sq_ready, n * 8 + (a + 1))
                    if a > 1:
                        pool.wait_ge(sq_read, n * 8 + (a - 8))
                    g.tensor_tensor(total_sq[:], sq[:, 0, :] if a == 1 else total_sq[:], sq[:, a % 2, :],
                                    ALU.add).then_inc(sq_read, 2 if a == 1 else 1)
                pool.wait_ge(rstd_step, n * 2 + 2)
                for a in range(A8):
                    g.tensor_tensor(dst[:, a, :], dst[:, a, :], rstd[:], ALU.mult).then_inc(norm_ready, 1)

            def load_h(n, dst, tile):
                pool.dma_start(dst[:], h_dram[tile]).then_inc(dev_in, 16)

            def store_sums(tile):
                last = Step(tile, 3, 1)
                for half in range(2):
                    pool.wait_ge(chunk_free, last.chunk(6 + 4 * (half + 1)) + NCHUNK)
                    pool.dma_start(h_dram[tile][:, 4 * half:4 * half + 4, :],
                                   acc[:, 4 * half:4 * half + 4, :]).then_inc(h2_half, 16)

            pool.wait_ge(h_stored, 16 * H_STORES)
            for tile in range(TT - 1):
                pool.wait_ge(x_lo, tile * 8 + 8)
                load_h(tile + 1, dev, tile + 1)
                job(tile + 1, dev)
                store_sums(tile)
                pool.wait_ge(h2_half, tile * 32 + 32)
                pool.dma_start(acc[:], h_dram[tile + 1]).then_inc(acc_in, 16)
                pool.wait_ge(acc_in, 16 * (tile + 1))
                pool.sem_inc(acc_tiles, 1)
            pool.wait_ge(x_lo, 8 * 4)
            load_h(4, dev, 0)
            job(4, dev)
            pool.wait_ge(x_lo, 8 * 5)
            load_h(5, dev, 1)
            job(5, dev)
            store_sums(TT - 1)
            pool.wait_ge(h2_half, 32 * TT)
            load_h(6, acc, 2)
            job(6, acc)
            pool.wait_ge(x_lo, 8 * 6)
            load_h(7, dev, 3)
            job(7, dev)

        @block.tensor
        def _(pe):
            mm = nc.tensor.matmul

            def three(out, wah, wal, bh, bl, start, stop):
                mm(out, wah, bh, start=start, stop=False)
                mm(out, wah, bl, start=False, stop=False)
                return mm(out, wal, bh, start=False, stop=stop)

            def first_norm():
                for a in range(A8):
                    last = mm(score_ps[0][:], mean_w[:], acc[:, a, :], start=(a == 0), stop=(a == A8 - 1))
                last.then_inc(mean_ready, 1)
                for a in range(A8):
                    pe.wait_ge(sq_ready, a + 1)
                    last = mm(score_ps[1][:], mean_w[:], sq[:, a % 2, :], start=(a == 0), stop=(a == A8 - 1))
                    last.then_inc(var_step, 1)

            def mean_of(n, units):
                pe.wait_ge(score_free, units + 2)
                pe.wait_ge(total_ready, n * 1)
                mm(score_ps[1][:], mean_w[:], total[:], start=True, stop=True).then_inc(mean_ready, 1)

            def variance_of(n):
                pe.wait_ge(sq_read, n * 8)
                pe.wait_ge(mean_read, n * 1)
                mm(score_ps[1][:], mean_w[:], total_sq[:], start=True, stop=True).then_inc(var_ready, 1)

            def project(st, m, j, x=None, x_count=None, midway=None):
                x = x or (xh[:], xl[:])
                pe.wait_ge(chunk_free, st.chunk(m) + 1)
                pe.wait_ge(w_lo, st.tile(j) + (NRAW + 1))
                slot = st.split_slot(j)
                for a in range(A8):
                    if midway is not None and a == A8 // 2:
                        midway()
                    if x_count is not None:
                        pe.wait_ge(x_lo, x_count + (a + 1))
                    w = slice(a * P, (a + 1) * P)
                    last = three(chunk_ps[st.bank(m)][:], wh[:, slot, w], wl[:, slot, w],
                                 x[0][:, a, :], x[1][:, a, :], a == 0, a == A8 - 1)
                last.then_inc(chunk_ready, 1)

            def turn_v(st):
                pe.wait_ge(chunk_free, st.chunk(1) + (NCHUNK + 1))
                pe.wait_ge(turn_free, st.heads() * 5 + 1)
                for u in range(CPT):
                    last = nc.tensor.transpose(turn_ps[:, u * P:(u + 1) * P], vt[:, u * P:(u + 1) * P], ident[:])
                last.then_inc(turn_ready, 1)

            def scores(st, u, job=None):
                if u == 0:
                    pe.wait_ge(r_lo, st.heads() * 5)
                pe.wait_ge(score_free, st.unit(u) + 1)
                if job is not None:
                    pe.wait_ge(mean_read, job * 1)
                tok = slice(u * SEQ, (u + 1) * SEQ)
                for h in range(GQ):
                    last = three(score_ps[u % 2][:, h * SEQ:(h + 1) * SEQ],
                                 qh[:, st.old, h, tok], ql[:, st.old, h, tok],
                                 kh[:, st.old, tok], kl[:, st.old, tok], True, True)
                last.then_inc(score_ready, 1)

            def turn_probs(st, u):
                pe.wait_ge(prob_ready, st.unit(u) + 1)
                pe.wait_ge(turn_free, st.heads() * 5 + (u - 3))
                for h in range(GQ):
                    last = nc.tensor.transpose(turn_ps[:, h * P:(h + 1) * P], prob[:, u % 2, h, :], ident[:])
                last.then_inc(turn_ready, 1)

            def attend(st, u):
                pe.wait_ge(turn_free, st.heads() * 5 + (u - 2))
                pe.wait_ge(attn_free, st.unit(u) + 1)
                keys = slice(u * P, (u + 1) * P)
                three(attn_ps[:], vh[:, st.old, keys], vl[:, st.old, keys],
                      pth[:], ptl[:], True, True).then_inc(attn_ready, 1)

            def wo_chunks(st, between=None):
                for o in range(A8):
                    pe.wait_ge(chunk_free, st.chunk(6 + o) + 1)
                    if o == 0:
                        pe.wait_ge(attn_free, st.unit(3) + 2)
                    slot = st.split_slot(6 + o // 2)
                    if o % 2 == 0:
                        pe.wait_ge(w_lo, st.tile(6 + o // 2) + (NRAW + 1))
                    for h in range(GQ):
                        w = slice(h * 256 + (o % 2) * P, h * 256 + (o % 2) * P + P)
                        last = three(chunk_ps[st.bank(6 + o)][:], wh[:, slot, w], wl[:, slot, w],
                                     oh[:, h, :], ol[:, h, :], h == 0, h == GQ - 1)
                    last.then_inc(chunk_ready, 1)
                    if between and o == between[0]:
                        between[1]()

            def step(st, x_count=None, job=None):
                if job is not None:
                    mean_of(job, st.unit(0))
                scores(st, 0)
                project(st, 0, 0, x_count=x_count)
                scores(st, 1, job)
                project(st, 1, 1, midway=lambda: turn_probs(st, 0))
                scores(st, 2)
                attend(st, 0)
                project(st, 2, 2, midway=lambda: turn_probs(st, 1))
                scores(st, 3)
                attend(st, 1)
                project(st, 3, 3, midway=lambda: turn_probs(st, 2))
                attend(st, 2)
                if st is LAST:
                    mean_of(5, st.unit(0) + 4)
                project(st, 4, 4, midway=lambda: turn_probs(st, 3))
                project(st, 5, 5, midway=lambda: attend(st, 3))
                if st is LAST:
                    wo_chunks(st, (7, lambda: variance_of(5)))
                    return
                turn_v(st)
                if job is not None:
                    variance_of(job)
                wo_chunks(st)

            def tile_steps(tile):
                with pe.Fori(0, 3) as it:
                    for q in range(2):
                        step(Step(tile, it, q))
                step(Step(tile, 3, 0), job=tile + 1)

            pe.wait_ge(in_const, 16 * 5)
            first_norm()
            for j in range(6):
                project(First(), j, j, x_count=0 if j == 0 else None)
            turn_v(First())
            with pe.Fori(0, TT - 1) as tile:
                tile_steps(tile)
                step(Step(tile, 3, 1), x_count=tile * 8 + 8)
            tile_steps(TT - 1)
            step(LAST, x_count=8 * 4)
            for c in range(6, TT * A8):
                t_, o = c // A8, c % A8
                if t_ in (1, 2) and o == 2:
                    mean_of(5 + t_, U_ALL)
                if t_ in (1, 2) and o == 6:
                    variance_of(5 + t_)
                project(LAST, *ffn_chunk(c), x=x_of(4 + t_), x_count=8 * (4 + t_) if o == 0 else None)

        @block.scalar
        def _(act):
            def copy(dst, src, done):
                nc.scalar.activation(dst, src, ACT.Copy).then_inc(done, 1)

            def weights(st, j):
                if not (isinstance(st, First) and j < NSPLIT):
                    act.wait_ge(chunk_ready, st.slot_free(j))
                act.wait_ge(raw_in[j % NRAW], st.raw_uses(j) * 16)
                copy(wh[:, st.split_slot(j), :], raw[:, j % NRAW, :], w_hi)

            def squares(n, src, read, some=range(A8)):
                for a in some:
                    act.wait_ge(dev_ready, n * 8 + (a + 1))
                    if a >= 2:
                        act.wait_ge(read, n * 8 + (a - 1) if read is var_step else n * 8 + (a - 9))
                    nc.scalar.activation(sq[:, a % 2, :], src[:, a, :], ACT.Square).then_inc(sq_ready, 1)

            def read_mean(n):
                act.wait_ge(mean_ready, n * 1 + 1)
                copy(mean[:], score_ps[1][:], mean_read)

            def deviation(n):
                act.wait_ge(rstd_step, n * 2 + 1)
                nc.scalar.activation(rstd[:], rstd[:], ACT.Sqrt).then_inc(std_ready, 1)

            def x_high(n, dst, src, some):
                for a in some:
                    act.wait_ge(norm_ready, n * 8 + (a + 1))
                    copy(dst[0][:, a, :], src[:, a, :], x_hi)

            def rotate(st, j, m):
                act.wait_ge(chunk_ready, st.chunk(j) + 1)
                ps = chunk_ps[st.bank(j)]
                nc.scalar.activation(rot[0:64, :], ps[64:128, :], ACT.Copy)
                nc.scalar.activation(rot[64:128, :], ps[0:64, :], ACT.Copy).then_inc(rot_ready, 1)

            def rope_hi(st, j, m):
                act.wait_ge(rope_ready, st.heads() * 5 + (m + 1))
                dst = kh[:, st.new, :] if j == 0 else qh[:, st.new, j - 2, :]
                copy(dst, roped[:], r_hi)

            def v_split(st):
                act.wait_ge(turn_ready, st.heads() * 5 + 1)
                copy(vh[:, st.new, :], turn_ps[:], v_hi)

            def exps(st, u):
                act.wait_ge(max_ready, st.unit(u) + 1)
                for h in range(GQ):
                    x = prob[:, u % 2, h, :]
                    last = nc.scalar.activation(x, x, ACT.Exp, bias=stat[:, u % 2, 0, h:h + 1], scale=QSCALE,
                                                accum_out=stat[:, u % 2, 1, h:h + 1])
                last.then_inc(exp_ready, 1)

            def probs_hi(st, u):
                act.wait_ge(turn_ready, st.heads() * 5 + (u - 3))
                copy(pth[:], turn_ps[:], pt_hi)

            def attn_hi(st, u):
                act.wait_ge(attn_ready, st.unit(u) + 1)
                if u == 0:
                    act.wait_ge(chunk_ready, st.chunk(0))
                copy(oh[:, :, u * SEQ:(u + 1) * SEQ], attn_ps[:].rearrange("p (h s) -> p h s", h=GQ), o_hi)

            def step(st, job=None):
                ffn = st is LAST

                def some_squares(i):
                    if job is not None:
                        squares(job, dev, sq_read, range(2 * i, 2 * i + 2))

                if job is not None:
                    read_mean(job)
                weights(st, 3)
                exps(st, 0)
                if not ffn:
                    rotate(st, 0, 0)
                exps(st, 1)
                probs_hi(st, 0)
                weights(st, 4)
                if not ffn:
                    rope_hi(st, 0, 0)
                attn_hi(st, 0)
                probs_hi(st, 1)
                exps(st, 2)
                weights(st, 5)
                some_squares(0)
                if not ffn:
                    rotate(st, 2, 1)
                attn_hi(st, 1)
                probs_hi(st, 2)
                exps(st, 3)
                weights(st, 6)
                some_squares(1)
                if not ffn:
                    rope_hi(st, 2, 1)
                    rotate(st, 3, 2)
                attn_hi(st, 2)
                weights(st, 7)
                probs_hi(st, 3)
                some_squares(2)
                if ffn:
                    read_mean(5)
                else:
                    rope_hi(st, 3, 2)
                    rotate(st, 4, 3)
                weights(st, 8)
                attn_hi(st, 3)
                some_squares(3)
                if not ffn:
                    rope_hi(st, 4, 3)
                    rotate(st, 5, 4)
                    v_split(st)
                weights(st, 9)
                if ffn:
                    squares(5, dev, sq_read, range(0, 2))
                else:
                    rope_hi(st, 5, 4)
                weights(st, 10)
                if ffn:
                    squares(5, dev, sq_read, range(2, 5))
                if job is not None:
                    deviation(job)
                    x_high(job, (xh, xl), dev, range(0, 4))
                weights(st, 11)
                if ffn:
                    squares(5, dev, sq_read, range(5, 8))
                if job is not None:
                    x_high(job, (xh, xl), dev, range(4, 8))
                weights(st, 12)

            def tile_steps(tile):
                with act.Fori(0, 3) as it:
                    for q in range(2):
                        step(Step(tile, it, q))
                step(Step(tile, 3, 0), tile + 1)

            first, second = First(), Step(0, 0, 0)
            for j in range(NRAW):
                weights(first, j)
            squares(0, dev, var_step)
            deviation(0)
            x_high(0, (xh, xl), dev, range(A8))
            weights(first, NRAW)
            act.wait_ge(h_stored, 16 * H_STORES)
            for j in range(6):
                weights(*((first, j + 3) if j < 3 else (second, j - 3)))
                if j >= 1 and j - 1 != 1:
                    m = (0, None, 1, 2, 3, 4)[j - 1]
                    rotate(first, j - 1, m)
                    rope_hi(first, j - 1, m)
            rotate(first, 5, 4)
            v_split(first)
            rope_hi(first, 5, 4)
            with act.Fori(0, TT - 1) as tile:
                tile_steps(tile)
                step(Step(tile, 3, 1))
            tile_steps(TT - 1)
            step(LAST)
            for c in range(6, TT * A8):
                t_, o = c // A8, c % A8
                if c + 7 < 10 + TT * A8 - 6:
                    weights(LAST, c + 7)
                if c == 6:
                    deviation(5)
                if c == 7:
                    x_high(5, x_of(5), dev, range(A8))
                if t_ in (1, 2):
                    src = acc if t_ == 1 else dev
                    if o == 3:
                        read_mean(5 + t_)
                    if o == 4:
                        squares(5 + t_, src, sq_read)
                    if o == 6:
                        deviation(5 + t_)
                    if o == 7:
                        x_high(5 + t_, x_of(5 + t_), src, range(A8))

        @block.vector
        def _(dve):
            v = nc.vector

            def split_lo(dst, src, hi, done):
                v.tensor_tensor(dst, src, hi.bitcast(F32), ALU.subtract).then_inc(done, 1)

            def weights(st, j):
                slot = st.split_slot(j)
                dve.wait_ge(w_hi, st.tile(j) + 1)
                split_lo(wl[:, slot, :], raw[:, j % NRAW, :], wh[:, slot, :], w_lo)

            def deviation(n):
                if isinstance(n, int) and n == 0:
                    dve.wait_ge(var_step, A8)
                else:
                    dve.wait_ge(var_ready, n * 1)
                v.tensor_scalar(rstd[:], score_ps[1][:], EPS, None, ALU.add).then_inc(rstd_step, 1)

            def invert(n):
                dve.wait_ge(std_ready, n * 1 + 1)
                v.reciprocal(rstd[:], rstd[:]).then_inc(rstd_step, 1)

            def x_low(n, dst, src, some):
                for a in some:
                    dve.wait_ge(x_hi, n * 8 + (a + 1))
                    split_lo(dst[1][:, a, :], src[:, a, :], dst[0][:, a, :], x_lo)

            def first_norm():
                dve.wait_ge(mean_ready, 1)
                for a in range(A8):
                    v.tensor_tensor(dev[:, a, :], acc[:, a, :], score_ps[0][:], ALU.subtract).then_inc(dev_ready, 1)
                deviation(0)
                invert(0)
                dve.wait_ge(rstd_step, 2)
                for a in range(A8):
                    v.tensor_tensor(dev[:, a, :], dev[:, a, :], rstd[:], ALU.mult).then_inc(norm_ready, 1)
                    if a >= 1:
                        x_low(0, (xh, xl), dev, [a - 1])
                x_low(0, (xh, xl), dev, [A8 - 1])

            def rope(st, j, m):
                def seqs(x):
                    return x.rearrange("p (c s) -> p c s", c=CPT)

                def table(x):
                    return x[:].unsqueeze(1).broadcast_to([P, CPT, SEQ])

                ps = chunk_ps[st.bank(j)]
                dve.wait_ge(rot_ready, st.heads() * 5 + (m + 1))
                v.tensor_tensor(seqs(direct[:]), seqs(ps[:]), table(cos), ALU.mult).then_inc(chunk_free, 1)
                v.tensor_tensor(seqs(rot[:]), seqs(rot[:]), table(sin), ALU.mult).then_inc(rope_step, 1)
                dve.wait_ge(rope_step, st.heads() * 5 + (m + 1))
                v.tensor_tensor(roped[:], direct[:], rot[:], ALU.add).then_inc(rope_ready, 1)

            def rope_lo(st, j, m):
                dve.wait_ge(r_hi, st.heads() * 5 + (m + 1))
                hi, lo = (x[:, st.new, :] if j == 0 else y[:, st.new, j - 2, :] for x, y in ((kh, qh), (kl, ql)))
                split_lo(lo, roped[:], hi, r_lo)

            def v_copy(st):
                dve.wait_ge(chunk_ready, st.chunk(1) + 1)
                v.tensor_copy(vt[:], chunk_ps[st.bank(1)][:]).then_inc(chunk_free, 1)

            def v_split(st):
                dve.wait_ge(v_hi, st.heads() + 1)
                split_lo(vl[:, st.new, :], turn_ps[:], vh[:, st.new, :], turn_free)

            def maxima(st, u):
                dve.wait_ge(score_ready, st.unit(u) + 1)
                v.tensor_tensor(prob[:, u % 2], score_ps[u % 2][:].rearrange("p (h s) -> p h s", h=GQ),
                                mask[:].unsqueeze(1).broadcast_to([P, GQ, SEQ]), ALU.add).then_inc(score_free, 1)
                dve.wait_ge(score_free, st.unit(u) + 3)
                v.reduce_max(stat[:, u % 2, 0, :], prob[:, u % 2], mybir.AxisListType.X).then_inc(max_step, 1)
                dve.wait_ge(max_step, st.unit(u) + 1)
                v.tensor_scalar(stat[:, u % 2, 0, :], stat[:, u % 2, 0, :], -QSCALE, None,
                                ALU.mult).then_inc(max_ready, 1)

            def normalise(st, u):
                dve.wait_ge(exp_ready, st.unit(u) + 1)
                v.reciprocal(stat[:, u % 2, 2, :], stat[:, u % 2, 1, :]).then_inc(inv_step, 1)
                dve.wait_ge(inv_step, st.unit(u) + 1)
                v.tensor_tensor(prob[:, u % 2], prob[:, u % 2],
                                stat[:, u % 2, 2, :].unsqueeze(2).broadcast_to([P, GQ, SEQ]),
                                ALU.mult).then_inc(prob_ready, 1)

            def probs_lo(st, u):
                dve.wait_ge(pt_hi, st.unit(u) + 1)
                split_lo(ptl[:], turn_ps[:], pth[:], turn_free)

            def attn_lo(st, u):
                dve.wait_ge(o_hi, st.unit(u) + 1)
                tok = slice(u * SEQ, (u + 1) * SEQ)
                split_lo(ol[:, :, tok], attn_ps[:].rearrange("p (h s) -> p h s", h=GQ), oh[:, :, tok], attn_free)

            def add_chunk(st, o):
                if o == 0:
                    dve.wait_ge(acc_tiles, st.tile_no * 1 + 1)
                dve.wait_ge(chunk_ready, st.chunk(6 + o) + 1)
                v.tensor_tensor(acc[:, o, :], acc[:, o, :], chunk_ps[st.bank(6 + o)][:], ALU.add).then_inc(chunk_free, 1)

            def result(c):
                m, slot = ffn_chunk(c)[0], c % NRES
                dve.wait_ge(res_in[slot], 16 * (c // NRES + 1))
                dve.wait_ge(chunk_ready, LAST.chunk(m) + 1)
                v.scalar_tensor_tensor(res[:, slot, :], chunk_ps[LAST.bank(m)][:], bias[:, c % A8:c % A8 + 1],
                                       res[:, slot, :], ALU.add, ALU.add).then_inc(chunk_free, 1)

            def step(st, job=None):
                ffn = st is LAST
                maxima(st, 0)
                weights(st, 3)
                normalise(st, 0)
                maxima(st, 1)
                if ffn:
                    result(0)
                else:
                    rope(st, 0, 0)
                probs_lo(st, 0)
                normalise(st, 1)
                weights(st, 4)
                if not ffn:
                    rope_lo(st, 0, 0)
                maxima(st, 2)
                attn_lo(st, 0)
                probs_lo(st, 1)
                if ffn:
                    result(1)
                else:
                    v_copy(st)
                normalise(st, 2)
                weights(st, 5)
                maxima(st, 3)
                if ffn:
                    result(2)
                else:
                    rope(st, 2, 1)
                attn_lo(st, 1)
                probs_lo(st, 2)
                normalise(st, 3)
                weights(st, 6)
                if ffn:
                    result(3)
                else:
                    rope_lo(st, 2, 1)
                    rope(st, 3, 2)
                attn_lo(st, 2)
                weights(st, 7)
                probs_lo(st, 3)
                if ffn:
                    result(4)
                else:
                    rope_lo(st, 3, 2)
                    rope(st, 4, 3)
                weights(st, 8)
                attn_lo(st, 3)
                if not ffn:
                    rope_lo(st, 4, 3)
                    rope(st, 5, 4)
                    v_split(st)
                weights(st, 9)
                if ffn:
                    result(5)
                else:
                    rope_lo(st, 5, 4)
                for o in range(A8):
                    add_chunk(st, o)
                    if o == 1:
                        weights(st, 10)
                        if job is not None:
                            deviation(job)
                            invert(job)
                    if o == 3:
                        if job is not None:
                            x_low(job, (xh, xl), dev, range(0, 4))
                        weights(st, 11)
                    if o == 5:
                        if job is not None:
                            x_low(job, (xh, xl), dev, range(4, 8))
                        weights(st, 12)

            def tile_steps(tile):
                with dve.Fori(0, 3) as it:
                    for q in range(2):
                        step(Step(tile, it, q))
                step(Step(tile, 3, 0), tile + 1)

            for given, count in ((w_lo, NRAW), (chunk_free, NCHUNK), (turn_free, 1), (score_free, 2), (attn_free, 1),
                                 (acc_tiles, 1)):
                dve.sem_inc(given, count)
            dve.wait_ge(in_const, 16 * 5)
            first, second = First(), Step(0, 0, 0)
            for j in range(NRAW):
                weights(first, j)
            first_norm()
            weights(first, NRAW)
            for j in range(6):
                weights(*((first, j + 3) if j < 3 else (second, j - 3)))
                if j == 2:
                    v_copy(first)
                elif j >= 1:
                    m = (0, None, 1, 2, 3, 4)[j - 1]
                    rope(first, j - 1, m)
                    rope_lo(first, j - 1, m)
            rope(first, 5, 4)
            v_split(first)
            rope_lo(first, 5, 4)
            with dve.Fori(0, TT - 1) as tile:
                tile_steps(tile)
                step(Step(tile, 3, 1))
            tile_steps(TT - 1)
            step(LAST)
            for c in range(6, TT * A8):
                t_, o = c // A8, c % A8
                if c + 7 < 10 + TT * A8 - 6:
                    weights(LAST, c + 7)
                if c == 6:
                    deviation(5)
                    invert(5)
                if c == 7:
                    x_low(5, x_of(5), dev, range(A8))
                if t_ in (1, 2) and o == 6:
                    deviation(5 + t_)
                    invert(5 + t_)
                if t_ in (1, 2) and o == 7:
                    x_low(5 + t_, x_of(5 + t_), acc if t_ == 1 else dev, range(A8))
                result(c)


class Kept:

    def __init__(self, nc, ctx):
        def sb(name, shape):
            return ctx.enter_context(nc.sbuf_tensor(name, shape, F32))

        def sem(name):
            return ctx.enter_context(nc.semaphore(name))

        self.acc = sb("acc", [P, A8, NT])
        self.raw = sb("raw", [P, NRAW, D])
        self.cos, self.sin = sb("cos", [P, SEQ]), sb("sin", [P, SEQ])
        self.mask, self.ident = sb("mask", [P, SEQ]), sb("ident", [P, P])
        self.mean_w = sb("mean_w", [P, P])
        self.bias = sb("bias", [P, A8])
        self.h_stored, self.in_const = sem("h_stored"), sem("in_const")
        self.raw_in = [sem(f"raw_in{i}") for i in range(NRAW)]


def program(nc, ins, out_dram, h_dram, weff_dram):
    with ExitStack() as ctx:
        kept = Kept(nc, ctx)
        s4d_and_lora_fold(nc, ins, kept, h_dram, weff_dram)
        transformer(nc, ins, kept, h_dram, weff_dram, out_dram)


def constants():
    f = np.float32
    tab = np.concatenate([np.arange(B0), B0 * np.arange(B1), P * np.arange(A8)]).astype(f)
    inv_freq = f(1.0) / f(10000.0) ** (np.arange(0, HD, 2, dtype=f) / f(HD))
    freqs = np.arange(SEQ, dtype=f)[:, None] * inv_freq[None, :]
    emb = np.concatenate([freqs, freqs], axis=-1)
    cos, sin = np.cos(emb).astype(f).T, np.sin(emb).astype(f).T
    sign = np.where(np.arange(HD) < HD // 2, f(-1), f(1))[:, None]
    pos = np.arange(SEQ)
    return {
        "tab": np.broadcast_to(tab, (P, NTAB)).copy(),
        "cos": cos.copy(), "sin": (sin * sign).astype(f),
        "mask": np.where(pos[:, None] >= pos[None, :], f(0), np.finfo(f).min).astype(f),
        "ident": np.eye(P, dtype=f),
        "mean_w": np.full((P, P), 1.0 / D, f),
    }


def kernel(x, L0_tok_log_dt, L0_tok_B, L0_tok_inv_A_real, L0_tok_A_imag, L0_attn_wq, L0_attn_wk, L0_attn_wv,
           L0_attn_wo, L0_ffn_W, L0_ffn_bias, L0_ffn_A, L0_ffn_Bf, L0_ffn_coeffs, L0_ffn_scales):
    import concourse.bacc as bacc
    from concourse.bass_utils import run_bass_kernel_spmd

    def both(y):
        return np.concatenate([np.asarray(y).T] * 2, axis=0)

    c = np.asarray(x).transpose(3, 2, 1, 0)
    b = np.asarray(L0_tok_B)
    wq = np.asarray(L0_attn_wq).reshape(NKV, GQ, HD, A8, P)
    wk = np.asarray(L0_attn_wk).reshape(NKV, 1, HD, A8, P)
    wv = np.asarray(L0_attn_wv).reshape(NKV, 1, HD, A8, P)
    wqkv = np.concatenate([wk, wv, wq], axis=1).transpose(0, 1, 4, 3, 2).reshape(NKV, 6, P, D)
    wo = np.asarray(L0_attn_wo).reshape(4, 256, NKV, GQ, HD).transpose(2, 0, 4, 3, 1).reshape(NKV, 4, P, D)
    per_expert = [np.repeat(np.asarray(y), ER // 16).reshape(2, P).T for y in (L0_ffn_coeffs, L0_ffn_scales)]
    arrays = {
        "small": np.stack([np.broadcast_to(np.asarray(L0_tok_log_dt), (P, SEQ)), both(L0_tok_inv_A_real),
                           both(L0_tok_A_imag), both(b[..., 0]), both(b[..., 1])], axis=1),
        "coef": np.concatenate([c.transpose(1, 0, 2, 3)] * 2, axis=0),
        "lora_a": np.asarray(L0_ffn_A).reshape(2, P, D).transpose(1, 0, 2),
        "lora_b": np.asarray(L0_ffn_Bf).transpose(0, 2, 1).reshape(2, P, D).transpose(1, 0, 2),
        "lora_w": np.concatenate(per_expert, axis=1),
        "wt": np.asarray(L0_ffn_W).T.reshape(A8, P, D),
        "wqkv": wqkv, "wo": wo,
        "bias": np.asarray(L0_ffn_bias).reshape(A8, P).T,
    }
    arrays.update(constants())
    arrays = {k: np.ascontiguousarray(v) for k, v in arrays.items()}

    nc = bacc.Bacc("TRN2", target_bir_lowering=False, num_devices=1)
    ins = {k: nc.dram_tensor(f"in_{k}", v.shape, mybir.dt.from_np(v.dtype), kind="ExternalInput").ap()
           for k, v in arrays.items()}
    out = nc.dram_tensor("out_t", (TT, A8, P, NT), F32, kind="ExternalOutput").ap()
    h_dram = nc.dram_tensor("h_t", (TT, P, A8, NT), F32, kind="Internal").ap()
    weff = nc.dram_tensor("weff", (A8, P, A8, P), F32, kind="Internal").ap()
    program(nc, ins, out, h_dram, weff)
    r = run_bass_kernel_spmd(nc, [{f"in_{k}": v for k, v in arrays.items()}], core_ids=[0])
    y = r.results[0]["out_t"].reshape(TT, D, CPT, SEQ)
    return y.transpose(0, 2, 3, 1).reshape(NB, SEQ, D)
```

```python
import math
from contextlib import ExitStack

import numpy as np

import concourse.bass as bass
from concourse import mybir

F32 = mybir.dt.float32
F32R = mybir.dt.float32r
I32 = mybir.dt.int32
ALU = mybir.AluOpType
ACT = mybir.ActivationFunctionType

NB, SEQ, NS = 16, 128, 64
D = 1024
A8, P = D // 128, 128
HD, NKV, GQ = 128, 8, 4
TT = 4
NT = NB * SEQ // TT
CPT = NT // SEQ
QSCALE = 1.0 / math.sqrt(HD)
EPS = 1e-5
ER = 256

NRAW, NSPLIT = 2, 4
NCHUNK, NRES = 4, 4
U_ALL = TT * NKV * CPT
H_STORES = 2 * (TT - 1)

B0, B1 = 16, 8
NTAB = B0 + B1 + A8
HBLK = 8
DVE_POS = 2
LORA_FIRST = 13
MAGIC = 12582912.0
TWO_PI_LOW = 6.283185


def s4d_and_lora_fold(nc, ins, kept, h_dram, weff_dram):
    acc, h_stored, ident = kept.acc, kept.h_stored, kept.ident
    ctx = ExitStack()
    with ctx:
        def sb(name, shape, dt=F32):
            return ctx.enter_context(nc.sbuf_tensor(name, shape, dt))

        def sem(name):
            return ctx.enter_context(nc.semaphore(name))

        hbuf = sb("hbuf", [P, TT - 1, A8, NT])
        small = sb("small", [P, 5, SEQ])
        tab = sb("tab", [P, NTAB])
        coef = sb("coef", [P, 2, SEQ, NB])
        flat = hbuf[:].rearrange("p t a n -> p (t a n)")

        def big(i):
            return flat[:, i * SEQ * NTAB:(i + 1) * SEQ * NTAB].rearrange("p (s j) -> p s j", j=NTAB)

        turn, absturn, mag = big(0), big(1), big(2)
        cosr = sb("cosr", [P, SEQ, NTAB])
        sini = sb("sini", [P, SEQ, NTAB])
        x0 = sb("x0", [P, SEQ, B0])
        y0 = sb("y0", [P, SEQ, B0])
        wa = sb("wa", [P, SEQ, A8])
        wb = sb("wb", [P, SEQ, A8])
        w2a = sb("w2a", [P, 2, HBLK, P])
        w2b = sb("w2b", [P, 2, HBLK, P])
        pa = sb("pa", [P, 2, HBLK, P])
        pb = sb("pb", [P, 2, HBLK, P])
        ex = sb("ex", [P, 2, SEQ])
        t = sb("t", [P, 8, SEQ])
        ti = sb("ti", [P, 2, SEQ], I32)
        half_pi = sb("half_pi", [P, 1])
        lora_a = sb("lora_a", [P, 2, D])
        lora_b = sb("lora_b", [P, 2, D])
        lora_w = sb("lora_w", [P, 4])
        lora_wt = kept.raw[:, 0, :].rearrange("p (n o) -> p n o", n=2)
        lora_out = kept.raw[:, 1, :].rearrange("p (n o) -> p n o", n=2)
        banks = [ctx.enter_context(nc.psum_tensor(f"s4d{i}", [P, 512], F32)) for i in range(8)]

        in_small, in_coef = sem("in_small"), sem("in_coef")
        in_lora = sem("in_lora")
        in_wt = [sem(f"in_wt{i}") for i in range(2)]
        dve_done = sem("dve_done")
        act_done = sem("act_done")
        lora_b_ready = sem("lora_b_ready")
        lora_ready, lora_read = sem("lora_ready"), sem("lora_read")
        lora_stored = [sem(f"lora_stored{i}") for i in range(2)]
        table_part = sem("table_part")
        w2_mul, blk_ready, blk_used, h_read = sem("w2_mul"), sem("blk_ready"), sem("blk_used"), sem("h_read")
        pool_ready = sem("pool_ready")
        NBLK = SEQ // HBLK
        lora_after = {3 * i: LORA_FIRST + i for i in range(16 - LORA_FIRST)}
        marks = {}
        block = ctx.enter_context(nc.Block())

        tabs = tab[:].unsqueeze(1).broadcast_to([P, SEQ, NTAB])

        def rows(x):
            return x.unsqueeze(2).broadcast_to([P, SEQ, NTAB])

        def product(engine, n, dst, outer, inner, first, last):
            rows_o, rows_i = outer.shape[-1], inner.shape[-1]
            pos = slice(n * HBLK + first, n * HBLK + last)
            shape = [P, last - first, rows_o, rows_i]
            return engine.tensor_tensor(
                dst[:, n % 2, first:last].rearrange("p s (o i) -> p s o i", o=rows_o),
                outer[:, pos].unsqueeze(3).broadcast_to(shape),
                inner[:, pos].unsqueeze(2).broadcast_to(shape), ALU.mult)

        @block.sync
        def _(sp):
            sp.dma_start(small[:], ins["small"]).then_inc(in_small, 16)
            sp.dma_start(tab[:], ins["tab"]).then_inc(in_small, 16)
            sp.dma_start(lora_w[:], ins["lora_w"]).then_inc(in_lora, 16)
            sp.dma_start(ident[:], ins["ident"]).then_inc(in_lora, 16)
            sp.dma_start(lora_b[:], ins["lora_b"]).then_inc(in_lora, 16)
            sp.dma_start(lora_a[:], ins["lora_a"]).then_inc(in_lora, 16)

            def load_wt(n):
                a, oh = n // 2, n % 2
                sp.dma_start(lora_wt[:, n % 2, :], ins["wt"][a, :, oh * 512:(oh + 1) * 512]).then_inc(in_wt[n % 2], 16)

            load_wt(0)
            load_wt(1)
            sp.dma_start(coef[:], ins["coef"]).then_inc(in_coef, 16)
            for name, dst in (("cos", kept.cos), ("sin", kept.sin), ("mask", kept.mask),
                              ("mean_w", kept.mean_w), ("bias", kept.bias)):
                sp.dma_start(dst[:], ins[name]).then_inc(kept.in_const, 16)
            for n in range(16):
                a, oh = n // 2, n % 2
                if n + 1 < 16 and n >= 1:
                    sp.wait_ge(lora_ready, n)
                    load_wt(n + 1)
                sp.wait_ge(lora_read, n + 1)
                sp.dma_start(weff_dram[oh * 4:oh * 4 + 4, :, a, :].rearrange("t p o -> p t o"),
                             lora_out[:, n % 2, :].rearrange("p (t o) -> p t o", t=4)).then_inc(lora_stored[n % 2], 16)
            for i in range(2):
                sp.wait_ge(lora_stored[i], 16 * 8)
            for j in range(NRAW):
                sp.dma_start(kept.raw[:, j, :], ins["wqkv"][0, FIRST_ORDER[j]]).then_inc(kept.raw_in[j], 16)
            for half in range(2):
                s = slice(half * SEQ // 2, (half + 1) * SEQ // 2)
                sp.wait_ge(h_read, (half + 1) * SEQ // 8)
                for tile in range(1, TT):
                    sp.dma_start(h_dram[tile].rearrange("p a (c s) -> p (a c) s", c=CPT)[:, :, s],
                                 hbuf[:, tile - 1].rearrange("p a (c s) -> p (a c) s", c=CPT)[:, :, s]).then_inc(h_stored, 16)

        @block.vector
        def _(dve):
            n_done = [0]

            def link(ins_):
                n_done[0] += 1
                ins_.then_inc(dve_done, 1)
                dve.wait_ge(dve_done, n_done[0])

            v = nc.vector
            link(v.memset(half_pi[:], math.pi / 2))
            dve.wait_ge(in_small, 32)
            arg = small[:, 0:2, :]
            k2, r2, e2 = t[:, 0:2, :], t[:, 2:4, :], t[:, 4:6, :]
            link(v.tensor_scalar(k2, arg, 1.4426950408889634, MAGIC, ALU.mult, ALU.add))
            link(v.tensor_scalar(k2, k2, MAGIC, -126.0, ALU.subtract, ALU.max))
            link(v.tensor_scalar(k2, k2, 127.0, None, ALU.min))
            link(v.scalar_tensor_tensor(r2, k2, -0.693359375, arg, ALU.mult, ALU.add))
            link(v.scalar_tensor_tensor(r2, k2, 2.12194440e-4, r2, ALU.mult, ALU.add))
            link(v.tensor_scalar(ti[:], k2, 127.0, 8388608.0, ALU.add, ALU.mult))
            link(v.tensor_scalar(e2, r2, 1.0 / 5040, 1.0 / 720, ALU.mult, ALU.add))
            for c in (1.0 / 120, 1.0 / 24, 1.0 / 6, 0.5, 1.0):
                link(v.tensor_tensor(e2, e2, r2, ALU.mult))
                link(v.tensor_scalar(e2, e2, c, None, ALU.add))
            link(v.tensor_tensor(e2, e2, r2, ALU.mult))
            link(v.tensor_scalar(e2, e2, 1.0, None, ALU.add))
            link(v.tensor_tensor(ex[:], e2, ti[:].bitcast(F32), ALU.mult))
            dt, are = ex[:, 0, :], ex[:, 1, :]
            ar, theta, vturn, kk = t[:, 0, :], t[:, 1, :], t[:, 2, :], t[:, 3, :]
            link(v.scalar_tensor_tensor(ar, are, -1.0, dt, ALU.mult, ALU.mult))
            marks["decay"] = n_done[0]
            link(v.tensor_tensor(theta, small[:, 2, :], dt, ALU.mult))
            link(v.tensor_scalar(kk, theta, 1.0 / (2 * math.pi), MAGIC, ALU.mult, ALU.add))
            link(v.tensor_scalar(kk, kk, MAGIC, None, ALU.subtract))
            link(v.scalar_tensor_tensor(vturn, kk, -6.28125, theta, ALU.mult, ALU.add))
            link(v.scalar_tensor_tensor(vturn, kk, -0.0019353071795864769, vturn, ALU.mult, ALU.add))
            link(v.tensor_scalar(vturn, vturn, 1.0 / (2 * math.pi), None, ALU.mult))

            dve.wait_ge(in_lora, 64)
            link(v.tensor_tensor(lora_w[:, 0:2], lora_w[:, 0:2], lora_w[:, 2:4], ALU.mult))
            for k in range(2):
                ins_ = v.tensor_scalar(lora_b[:, k, :], lora_b[:, k, :], lora_w[:, k:k + 1], None, ALU.mult)
                ins_.then_inc(lora_b_ready, 1)
            link(v.tensor_tensor(turn, rows(vturn), tabs, ALU.mult))
            link(v.tensor_scalar(absturn, turn, MAGIC, None, ALU.add))
            link(v.scalar_tensor_tensor(turn, absturn, MAGIC, turn, ALU.subtract, ALU.subtract))
            marks["turn"] = n_done[0]
            link(v.scalar_tensor_tensor(absturn, turn, -1.0, turn, ALU.mult, ALU.max))
            marks["abs"] = n_done[0]
            em, lim, mask = t[:, 4, :], t[:, 5, :], ti[:, 0, :]
            link(v.tensor_scalar(lim, ar, -0.5, None, ALU.max))
            link(v.tensor_scalar(em, lim, 1.0 / 40320, 1.0 / 5040, ALU.mult, ALU.add))
            for c in (1.0 / 720, 1.0 / 120, 1.0 / 24, 1.0 / 6, 0.5, 1.0):
                link(v.tensor_tensor(em, em, lim, ALU.mult))
                link(v.tensor_scalar(em, em, c, None, ALU.add))
            link(v.tensor_tensor(em, em, lim, ALU.mult))
            link(v.tensor_scalar(mask, ar, -0.5, None, ALU.is_lt))
            dve.wait_ge(act_done, 4)
            link(v.tensor_scalar(lim, mag[:, :, 1], -1.0, None, ALU.add))
            link(v.copy_predicated(em, mask, lim))
            s1, c1, sh = sini[:, :, 1], cosr[:, :, 1], t[:, 3, :]
            c1m, er, ei = t[:, 5, :], t[:, 6, :], t[:, 7, :]
            link(v.scalar_tensor_tensor(c1m, sh, -2.0, sh, ALU.mult, ALU.mult))
            link(v.tensor_tensor(er, em, c1, ALU.mult))
            link(v.tensor_tensor(er, er, c1m, ALU.add))
            link(v.scalar_tensor_tensor(ei, em, 1.0, s1, ALU.add, ALU.mult))
            aim, den, tmp = small[:, 2, :], t[:, 0, :], t[:, 1, :]
            link(v.tensor_tensor(den, are, are, ALU.mult))
            link(v.tensor_tensor(tmp, aim, aim, ALU.mult))
            link(v.tensor_tensor(den, den, tmp, ALU.add))
            link(v.reciprocal(den, den))
            link(v.tensor_scalar(den, den, 2.0, None, ALU.mult))
            xq, yq = t[:, 2, :], t[:, 3, :]
            link(v.tensor_tensor(xq, ei, aim, ALU.mult))
            link(v.tensor_tensor(tmp, er, are, ALU.mult))
            link(v.tensor_tensor(xq, xq, tmp, ALU.subtract))
            link(v.tensor_tensor(xq, xq, den, ALU.mult))
            link(v.tensor_tensor(yq, ei, are, ALU.mult))
            link(v.tensor_tensor(tmp, er, aim, ALU.mult))
            link(v.tensor_tensor(yq, yq, tmp, ALU.add))
            link(v.scalar_tensor_tensor(yq, yq, -1.0, den, ALU.mult, ALU.mult))
            gr, gi = t[:, 4, :], t[:, 5, :]
            br, bi = small[:, 3, :], small[:, 4, :]
            link(v.tensor_tensor(gr, xq, br, ALU.mult))
            link(v.tensor_tensor(tmp, yq, bi, ALU.mult))
            link(v.tensor_tensor(gr, gr, tmp, ALU.subtract))
            link(v.tensor_tensor(gi, xq, bi, ALU.mult))
            link(v.tensor_tensor(tmp, yq, br, ALU.mult))
            link(v.tensor_tensor(gi, gi, tmp, ALU.add))
            rest = slice(B0, NTAB)
            link(v.tensor_tensor(cosr[:, :, rest], cosr[:, :, rest], mag[:, :, rest], ALU.mult))
            link(v.tensor_tensor(sini[:, :, rest], sini[:, :, rest], mag[:, :, rest], ALU.mult))

            def eight(x):
                return x.unsqueeze(2).broadcast_to([P, SEQ, A8])

            rot, iot = cosr[:, :, B0 + B1:NTAB], sini[:, :, B0 + B1:NTAB]

            def scratch(x):
                return x[:, 0].rearrange("p s q -> p (s q)").rearrange("p (s a) -> p s a", a=A8)

            grr, gii, tm = scratch(pa), scratch(pb), scratch(w2a)
            link(v.tensor_tensor(grr, rot, eight(gr), ALU.mult))
            link(v.tensor_tensor(tm, iot, eight(gi), ALU.mult))
            link(v.tensor_tensor(grr, grr, tm, ALU.subtract))
            link(v.tensor_tensor(gii, rot, eight(gi), ALU.mult))
            link(v.tensor_tensor(tm, iot, eight(gr), ALU.mult))
            link(v.tensor_tensor(gii, gii, tm, ALU.add))
            hr, hi = slice(0, 64), slice(64, 128)
            link(v.tensor_copy(wa[hr], grr[hr]))
            link(v.tensor_scalar(wa[hi], gii[hi], -1.0, None, ALU.mult))
            link(v.tensor_scalar(wb[hr], gii[hr], -1.0, None, ALU.mult))
            link(v.tensor_scalar(wb[hi], grr[hi], -1.0, None, ALU.mult))
            marks["weights"] = n_done[0]
            dve.wait_ge(in_coef, 16)
            dve.wait_ge(table_part, 5)
            dve.wait_ge(act_done, 5)

            for n in range(NBLK):
                d = n % 2
                if n >= 2:
                    dve.wait_ge(blk_used, n - 1)
                product(v, n, w2a, cosr[:, :, B0:B0 + B1], x0, 0, HBLK)
                product(v, n, w2b, sini[:, :, B0:B0 + B1], y0, 0, HBLK).then_inc(w2_mul, 1)
                product(v, n, pa, coef[:, 0], wa, 0, DVE_POS)
                dve.wait_ge(w2_mul, n + 1)
                v.tensor_tensor(w2a[:, d], w2a[:, d], w2b[:, d], ALU.add).then_inc(blk_ready, 1)

        @block.gpsimd
        def _(pool):
            g = nc.gpsimd
            pool.wait_ge(in_small, 32)
            pool.wait_ge(dve_done, marks["decay"])
            g.tensor_tensor(mag, rows(t[:, 0, :]), tabs, ALU.mult).then_inc(table_part, 1)
            pool.wait_ge(act_done, 3)
            lower, upper = slice(0, 64), slice(64, 128)
            for i, (dst, part, table) in enumerate(((y0, lower, sini), (x0, lower, cosr),
                                                    (x0, upper, sini), (y0, upper, cosr))):
                pool.wait_ge(table_part, i + 1)
                g.tensor_tensor(dst[part], table[part, :, 0:B0], mag[part, :, 0:B0], ALU.mult).then_inc(table_part, 1)
            pool.wait_ge(in_coef, 16)
            pool.wait_ge(dve_done, marks["weights"])
            pool.wait_ge(table_part, 5)
            for n in range(NBLK):
                if n >= 2:
                    pool.wait_ge(blk_used, n - 1)
                product(g, n, pb, coef[:, 1], wb, 0, HBLK)
                product(g, n, pa, coef[:, 0], wa, DVE_POS, HBLK).then_inc(pool_ready, 1)

        @block.scalar
        def _(act):
            def lora_copies(some):
                for n in some:
                    act.wait_ge(lora_ready, n + 1)
                    if n >= 2:
                        act.wait_ge(lora_stored[n % 2], 16 * (n // 2))
                    nc.scalar.activation(lora_out[:, n % 2, :], banks[n % 2][:], ACT.Copy).then_inc(lora_read, 1)

            act.wait_ge(table_part, 1)
            nc.scalar.activation(mag, mag, ACT.Exp).then_inc(act_done, 1)
            lora_copies(range(0, 1))
            act.wait_ge(dve_done, marks["turn"])
            nc.scalar.activation(sini[:], turn, ACT.Sin, scale=-TWO_PI_LOW).then_inc(act_done, 1)
            lora_copies(range(1, 2))
            act.wait_ge(dve_done, marks["abs"])
            nc.scalar.activation(cosr[:], absturn, ACT.Sin, bias=half_pi[:], scale=-TWO_PI_LOW).then_inc(act_done, 1)
            nc.scalar.activation(t[:, 3, :], turn[:, :, 1], ACT.Sin, scale=TWO_PI_LOW / 2).then_inc(act_done, 1)
            lora_copies(range(2, 6))
            act.wait_ge(table_part, 2)
            nc.scalar.activation(y0[0:64], y0[0:64], ACT.Copy, scale=-1.0).then_inc(act_done, 1)
            lora_copies(range(6, LORA_FIRST))
            for n in range(SEQ // 4):
                act.wait_ge(blk_used, n // 2 + 1)
                s = slice(4 * n, 4 * n + 4)
                got = banks[2 + n % 6][:].rearrange("p (s c a) -> p s c a", s=4, a=A8)
                for tile in range(TT):
                    dst = (hbuf[:, tile - 1] if tile else acc[:]).rearrange("p a (c s) -> p s c a", c=CPT)
                    last = nc.scalar.activation(dst[:, s], got[:, :, tile * CPT:(tile + 1) * CPT], ACT.Copy)
                last.then_inc(h_read, 1)
                if n % 2 == 1 and n // 2 in lora_after:
                    lora_copies([lora_after[n // 2]])

        @block.tensor
        def _(pe):
            pe.wait_ge(in_lora, 64)
            pe.wait_ge(lora_b_ready, 2)

            def lora_tile(n):
                a, oh = n // 2, n % 2
                if n >= 2:
                    pe.wait_ge(lora_read, n - 1)
                for k in range(2):
                    nc.tensor.matmul(banks[n % 2][:], lora_a[:, k, a * P:(a + 1) * P],
                                     lora_b[:, k, oh * 512:(oh + 1) * 512], start=(k == 0), stop=False)
                pe.wait_ge(in_wt[n % 2], 16 * (n // 2 + 1))
                nc.tensor.matmul(banks[n % 2][:], ident[:], lora_wt[:, n % 2, :],
                                 start=False, stop=True).then_inc(lora_ready, 1)

            for n in range(LORA_FIRST):
                lora_tile(n)
            for n in range(NBLK):
                pe.wait_ge(blk_ready, n + 1)
                pe.wait_ge(pool_ready, n + 1)
                for half in range(2):
                    m = 2 * n + half
                    if m >= 6:
                        pe.wait_ge(h_read, m - 5)
                    for j in range(4):
                        s = half * 4 + j
                        out = banks[2 + m % 6][:, j * P:(j + 1) * P]
                        nc.tensor.matmul(out, w2a[:, n % 2, s, :], pa[:, n % 2, s, :], start=True, stop=False)
                        last = nc.tensor.matmul(out, w2a[:, n % 2, s, :], pb[:, n % 2, s, :], start=False, stop=True)
                last.then_inc(blk_used, 1)
                if n in lora_after:
                    lora_tile(lora_after[n])


class Step:

    def __init__(self, tile, it, q):
        self.tile_no, self.it, self.q = tile, it, q
        self.new, self.old = 1 - q, q

    def at(self, each, rest):
        value = each * (1 + self.q) + rest
        for factor, variable in ((8 * each, self.tile_no), (2 * each, self.it)):
            value = variable * factor + value
        return value

    def tile(self, j):
        return self.at(10, j - 4)

    def split_slot(self, j):
        return (10 * (1 + self.q) - 4 + j) % NSPLIT

    def raw_uses(self, j):
        return self.at(10 // NRAW, (j - 4) // NRAW + 1)

    def slot_free(self, j):
        return self.chunk(j - 3 if j < 10 else 8 + 2 * (j - 10) if j < 14 else j + 1)

    def chunk(self, m):
        return self.at(14, m - 8)

    def bank(self, m):
        return (14 * (1 + self.q) - 8 + m) % NCHUNK

    def unit(self, u):
        return self.at(4, u - 4)

    def heads(self):
        return self.at(1, 0)


FIRST_ORDER = (0, 2, 3, 4, 5, 1)


class First(Step):

    def __init__(self):
        self.new = 0

    def tile(self, j):
        return j

    def split_slot(self, j):
        return j % NSPLIT

    def raw_uses(self, j):
        return j // NRAW + 1

    def slot_free(self, j):
        return j - 3

    def chunk(self, m):
        return FIRST_ORDER.index(m)

    def bank(self, m):
        return self.chunk(m) % NCHUNK

    def heads(self):
        return 0


LAST = Step(TT - 1, 3, 1)
LAST7 = Step(TT - 1, 3, 0)


def ffn_chunk(c):
    return (c, c) if c < 6 else (c + 8, c + 4)


def mean_at(job):
    return 11 + 8 * (job - 6)


def transformer(nc, ins, kept, h_dram, weff_dram, out_dram):
    acc, raw, h_stored, in_const, raw_in = kept.acc, kept.raw, kept.h_stored, kept.in_const, kept.raw_in
    cos, sin, mask, ident, mean_w, bias = kept.cos, kept.sin, kept.mask, kept.ident, kept.mean_w, kept.bias
    ctx = ExitStack()
    with ctx:
        def sb(name, shape, dt=F32):
            return ctx.enter_context(nc.sbuf_tensor(name, shape, dt))

        def sem(name):
            return ctx.enter_context(nc.semaphore(name))

        qh, ql = sb("qh", [P, 2, GQ, NT], F32R), sb("ql", [P, 2, GQ, NT], F32R)
        khl = sb("khl", [P, 2, 2, NT], F32R)
        kh, kl = khl[:, :, 0, :], khl[:, :, 1, :]
        vh, vl = sb("vh", [P, 2, NT], F32R), sb("vl", [P, 2, NT], F32R)
        dev = sb("dev", [P, A8, NT])
        sq = sb("sq", [P, 2, NT])
        total, total_sq = sb("total", [P, NT]), sb("total_sq", [P, NT])
        mean = sb("mean", [P, NT])
        rstd = sb("rstd", [P, NT])
        xh, xl = sb("xh", [P, A8, NT], F32R), sb("xl", [P, A8, NT], F32R)
        wh, wl = sb("wh", [P, NSPLIT, D], F32R), sb("wl", [P, NSPLIT, D], F32R)
        vt = sb("vt", [P, NT])
        rot, direct, roped = sb("rot", [P, NT]), sb("direct", [P, NT]), sb("roped", [P, NT])
        prob = sb("prob", [P, 2, GQ, SEQ])
        stat = sb("stat", [P, 2, 3, GQ])
        pth, ptl = sb("pth", [P, NT], F32R), sb("ptl", [P, NT], F32R)
        oh, ol = sb("oh", [P, GQ, NT], F32R), sb("ol", [P, GQ, NT], F32R)
        res = sb("res", [P, NRES, NT])

        chunk_ps = [ctx.enter_context(nc.psum_tensor(f"chunk{i}", [P, NT], F32)) for i in range(NCHUNK)]
        score_ps = ctx.enter_context(nc.psum_tensor("score", [P, 2, NT], F32))
        score_of = score_ps[:].rearrange("p b (h z s) -> p (b h) z s", h=2, z=2)
        mean_ps, var_ps = score_ps[:, 0, :], score_ps[:, 1, :]
        turn_ps = ctx.enter_context(nc.psum_tensor("turn", [P, NT], F32))
        attn_ps = ctx.enter_context(nc.psum_tensor("attn", [P, NT], F32))

        w_hi = sem("w_hi")
        w_lo = sem("w_lo")
        chunk_ready, chunk_free = sem("chunk_ready"), sem("chunk_free")
        rot_ready, rope_step, rope_ready = sem("rot_ready"), sem("rope_step"), sem("rope_ready")
        r_hi, r_lo = sem("r_hi"), sem("r_lo")
        turn_ready, turn_free = sem("turn_ready"), sem("turn_free")
        v_hi = sem("v_hi")
        score_ready, score_free = sem("score_ready"), sem("score_free")
        mask_step = sem("mask_step")
        max_step, max_ready, exp_ready = sem("max_step"), sem("max_ready"), sem("exp_ready")
        inv_step, prob_ready = sem("inv_step"), sem("prob_ready")
        pt_hi = sem("pt_hi")
        attn_ready, attn_free = sem("attn_ready"), sem("attn_free")
        o_hi = sem("o_hi")
        dev_in = sem("dev_in")
        last_in = sem("last_in")
        acc_in = sem("acc_in")
        acc_tiles = sem("acc_tiles")
        h2_half = sem("h2_half")
        sum_step, total_ready = sem("sum_step"), sem("total_ready")
        mean_ready, mean_read = sem("mean_ready"), sem("mean_read")
        dev_ready, sq_ready, sq_read = sem("dev_ready"), sem("sq_ready"), sem("sq_read")
        var_step, var_ready, rstd_step, std_ready = sem("var_step"), sem("var_ready"), sem("rstd_step"), sem("std_ready")
        first_sum, first_odd = sem("first_sum"), sem("first_odd")
        norm_ready, x_hi, x_lo = sem("norm_ready"), sem("x_hi"), sem("x_lo")
        res_in = [sem(f"res_in{i}") for i in range(NRES)]
        res_out = [sem(f"res_out{i}") for i in range(NRES)]

        q_as_x = [t_[:].rearrange("p z h s -> p (z h) s") for t_ in (qh, ql)]

        def x_of(job):
            return q_as_x if job in (5, 7) else (xh[:], xl[:])

        def sums(engine, waits, n, dst):
            if isinstance(n, int) and n == 7:
                waits.wait_ge(last_in, 16)
            else:
                waits.wait_ge(dev_in, n * 16)
            for a in range(1, A8):
                if a > 1:
                    waits.wait_ge(sum_step, n * 6 + (a - 7))
                ins_ = engine.tensor_tensor(total[:], dst[:, 0, :] if a == 1 else total[:], dst[:, a, :], ALU.add)
                ins_.then_inc(total_ready if a == A8 - 1 else sum_step, 1)

        def square_sums(engine, waits, n, some=range(1, A8)):
            for a in some:
                waits.wait_ge(sq_ready, n * 8 + (a + 1))
                if a > 1:
                    waits.wait_ge(sq_read, n * 8 + (a - 8))
                engine.tensor_tensor(total_sq[:], sq[:, 0, :] if a == 1 else total_sq[:], sq[:, a % 2, :],
                                     ALU.add).then_inc(sq_read, 2 if a == 1 else 1)

        block = ctx.enter_context(nc.Block())

        @block.sync
        def _(sp):
            def load(st, j, src):
                sp.wait_ge(w_lo, st.tile(j) + 1)
                sp.dma_start(raw[:, j % NRAW, :], src).then_inc(raw_in[j % NRAW], 16)

            def step_loads(st, new, old):
                for j in range(6):
                    load(st, j, ins["wqkv"][new, j])
                for j in range(4):
                    load(st, 6 + j, ins["wo"][old, j])

            def tile_loads(tile):
                with sp.Fori(0, 3) as it:
                    for q in range(2):
                        step_loads(Step(tile, it, q), it * 2 + (1 + q), it * 2 + q)
                step_loads(Step(tile, 3, 0), 7, 6)

            for j in range(NRAW, 6):
                load(First(), j, ins["wqkv"][0, FIRST_ORDER[j]])
            with sp.Fori(0, TT - 1) as tile:
                tile_loads(tile)
                step_loads(Step(tile, 3, 1), 0, 7)
            tile_loads(TT - 1)

            def tile_of(slot):
                if 6 <= slot < 10:
                    return ins["wo"][NKV - 1, slot - 6]
                c = slot if slot < 6 else slot - 4
                return weff_dram[c % A8].rearrange("p a o -> p (a o)")

            def residual(c):
                t_, o, slot = c // A8, c % A8, c % NRES
                if c >= NRES:
                    sp.wait_ge(res_out[slot], 16 * (c // NRES))
                if c % A8 == 0:
                    sp.wait_ge(h2_half, 32 * (t_ + 1))
                sp.dma_start(res[:, slot, :], h_dram[t_][:, o, :]).then_inc(res_in[slot], 16)

            def store(c):
                slot = c % NRES
                sp.wait_ge(chunk_free, LAST.chunk(ffn_chunk(c)[0]) + (NCHUNK + 1))
                sp.dma_start(out_dram[c // A8, c % A8], res[:, slot, :]).then_inc(res_out[slot], 16)

            slots = 10 + TT * A8 - 6
            for j in range(5):
                load(LAST, j, tile_of(j))
            residual(0)
            for slot in range(slots + 1):
                if slot < 6 or 10 <= slot < slots - 1:
                    residual(slot + 1 if slot < 6 else slot - 3)
                if slot + 5 < slots:
                    load(LAST, slot + 5, tile_of(slot + 5))
                if 1 <= slot < 7 or 10 < slot:
                    store(slot - 1 if slot < 7 else slot - 5)
            for slot in range(NRES):
                sp.wait_ge(res_out[slot], 16 * (TT * A8 // NRES))

        @block.gpsimd
        def _(pool):
            g = nc.gpsimd

            def centre(n, dst):
                pool.wait_ge(mean_read, n)
                for a in range(A8):
                    g.tensor_tensor(dst[:, a, :], dst[:, a, :], mean[:], ALU.subtract).then_inc(dev_ready, 1)

            def normalise(n, dst, some=range(A8)):
                pool.wait_ge(rstd_step, n * 2 + 2)
                for a in some:
                    g.tensor_tensor(dst[:, a, :], dst[:, a, :], rstd[:], ALU.mult).then_inc(norm_ready, 1)

            def job(n, dst):
                sums(g, pool, n, dst)
                centre(n, dst)
                square_sums(g, pool, n)
                normalise(n, dst)

            def load_h(n, dst, tile):
                landed = last_in if n == 7 else dev_in
                pool.dma_start(dst, h_dram[tile]).then_inc(landed, 16)

            def store_sums(tile):
                last = Step(tile, 3, 1)
                for half in range(2):
                    pool.wait_ge(chunk_free, last.chunk(6 + 4 * (half + 1)) + NCHUNK)
                    pool.dma_start(h_dram[tile][:, 4 * half:4 * half + 4, :],
                                   acc[:, 4 * half:4 * half + 4, :]).then_inc(h2_half, 16)

            pool.wait_ge(rstd_step, 2)
            for a in range(1, A8, 2):
                g.tensor_tensor(dev[:, a, :], dev[:, a, :], rstd[:], ALU.mult).then_inc(first_odd, 1)
            pool.wait_ge(h_stored, 16 * H_STORES)
            for tile in range(TT - 1):
                pool.wait_ge(x_lo, tile * 8 + 8)
                if tile == 0:
                    pool.wait_ge(chunk_ready, 6)
                load_h(tile + 1, dev[:], tile + 1)
                job(tile + 1, dev)
                store_sums(tile)
                pool.wait_ge(h2_half, tile * 32 + 32)
                pool.dma_start(acc[:], h_dram[tile + 1]).then_inc(acc_in, 16)
                pool.wait_ge(acc_in, 16 * (tile + 1))
                pool.sem_inc(acc_tiles, 1)
            pool.wait_ge(x_lo, 8 * 4)
            load_h(4, dev[:], 0)
            job(4, dev)
            pool.wait_ge(x_lo, 8 * 5)
            load_h(5, dev[:], 1)
            job_5_stored = 5
            sums(g, pool, 5, dev)
            centre(5, dev)
            square_sums(g, pool, 5)
            store_sums(TT - 1)
            normalise(5, dev, range(job_5_stored))
            pool.wait_ge(h2_half, 32 * TT)
            load_h(6, acc[:], 2)
            normalise(5, dev, range(job_5_stored, A8))
            pool.wait_ge(x_lo, 8 * 6)
            centre(6, acc)
            load_h(7, dev[:], 3)
            normalise(6, acc)
            centre(7, dev)
            normalise(7, dev)

        @block.tensor
        def _(pe):
            mm = nc.tensor.matmul

            def three(out, wah, wal, bh, bl, start, stop):
                mm(out, wah, bh, start=start, stop=False)
                mm(out, wah, bl, start=False, stop=False)
                return mm(out, wal, bh, start=False, stop=stop)

            def first_norm():
                for a in range(A8 // 2):
                    mm(mean_ps, mean_w[:], acc[:, a, :], start=(a == 0), stop=False)
                pe.wait_ge(first_sum, A8 // 2 - 1)
                mm(mean_ps, mean_w[:], total[:], start=False, stop=True).then_inc(mean_ready, 1)
                for a in range(A8):
                    pe.wait_ge(sq_ready, a + 1)
                    last = mm(var_ps, mean_w[:], sq[:, a % 2, :], start=(a == 0), stop=(a == A8 - 1))
                    last.then_inc(var_step, 1)

            def mean_of(n, units):
                pe.wait_ge(score_free, units + 1)
                pe.wait_ge(total_ready, n)
                mm(mean_ps, mean_w[:], total[:], start=True, stop=True).then_inc(mean_ready, 1)

            def variance_of(n, units):
                pe.wait_ge(sq_read, n * 8)
                pe.wait_ge(score_free, units + 1)
                mm(var_ps, mean_w[:], total_sq[:], start=True, stop=True).then_inc(var_ready, 1)

            def project(st, m, j, x=None, x_count=None, midway=None):
                x = x or (xh[:], xl[:])
                pe.wait_ge(chunk_free, st.chunk(m) + 1)
                pe.wait_ge(w_lo, st.tile(j) + (NRAW + 1))
                slot = st.split_slot(j)
                for a in range(A8):
                    if midway is not None and a == A8 // 2:
                        midway()
                    if x_count is not None:
                        pe.wait_ge(x_lo, x_count + (a + 1))
                    w = slice(a * P, (a + 1) * P)
                    last = three(chunk_ps[st.bank(m)][:], wh[:, slot, w], wl[:, slot, w],
                                 x[0][:, a, :], x[1][:, a, :], a == 0, a == A8 - 1)
                last.then_inc(chunk_ready, 1)

            def turn_v(st):
                pe.wait_ge(chunk_free, st.chunk(1) + (NCHUNK + 1))
                pe.wait_ge(turn_free, st.heads() * 5 + 1)
                for u in range(CPT):
                    last = nc.tensor.transpose(turn_ps[:, u * P:(u + 1) * P], vt[:, u * P:(u + 1) * P], ident[:])
                last.then_inc(turn_ready, 1)

            def scores(st, u, mean_job=None, var_job=None):
                if u == 0:
                    pe.wait_ge(r_lo, st.heads() * 5)
                pe.wait_ge(score_free, st.unit(u) + 1)
                if mean_job is not None:
                    pe.wait_ge(mean_read, mean_job * 1)
                if var_job is not None:
                    pe.wait_ge(rstd_step, var_job * 2 + 1)
                tok = slice(u * SEQ, (u + 1) * SEQ)
                for h in range(GQ):
                    mm(score_of[:, h], qh[:, st.old, h, tok], khl[:, st.old, :, tok], start=True, stop=False)
                    last = mm(score_of[:, h, 0], ql[:, st.old, h, tok], kh[:, st.old, tok], start=False, stop=True)
                last.then_inc(score_ready, 1)

            def turn_probs(st, u):
                pe.wait_ge(prob_ready, st.unit(u) + 1)
                pe.wait_ge(turn_free, st.heads() * 5 + (u - 3))
                for h in range(GQ):
                    last = nc.tensor.transpose(turn_ps[:, h * P:(h + 1) * P], prob[:, u % 2, h, :], ident[:])
                last.then_inc(turn_ready, 1)

            def attend(st, u):
                pe.wait_ge(turn_free, st.heads() * 5 + (u - 2))
                pe.wait_ge(attn_free, st.unit(u) + 1)
                keys = slice(u * P, (u + 1) * P)
                three(attn_ps[:], vh[:, st.old, keys], vl[:, st.old, keys],
                      pth[:], ptl[:], True, True).then_inc(attn_ready, 1)

            def wo_chunks(st, between=None):
                for o in range(A8):
                    pe.wait_ge(chunk_free, st.chunk(6 + o) + 1)
                    if o == 0:
                        pe.wait_ge(attn_free, st.unit(3) + 2)
                    slot = st.split_slot(6 + o // 2)
                    if o % 2 == 0:
                        pe.wait_ge(w_lo, st.tile(6 + o // 2) + (NRAW + 1))
                    for h in range(GQ):
                        w = slice(h * 256 + (o % 2) * P, h * 256 + (o % 2) * P + P)
                        last = three(chunk_ps[st.bank(6 + o)][:], wh[:, slot, w], wl[:, slot, w],
                                     oh[:, h, :], ol[:, h, :], h == 0, h == GQ - 1)
                    last.then_inc(chunk_ready, 1)
                    if between and o == between[0]:
                        between[1]()

            def step(st, x_job=None, job=None):
                scores(st, 0, var_job=x_job)
                project(st, 0, 0, x_count=None if x_job is None else x_job * 8,
                        midway=None if job is None else lambda: mean_of(job, st.unit(0) + 1))
                scores(st, 1, mean_job=job)
                project(st, 1, 1, midway=lambda: turn_probs(st, 0))
                scores(st, 2)
                attend(st, 0)
                project(st, 2, 2, midway=lambda: turn_probs(st, 1))
                scores(st, 3)
                attend(st, 1)
                project(st, 3, 3, midway=lambda: turn_probs(st, 2))
                attend(st, 2)
                if st is LAST:
                    mean_of(5, st.unit(0) + 4)
                project(st, 4, 4, midway=lambda: turn_probs(st, 3))
                project(st, 5, 5, midway=lambda: attend(st, 3))
                if st is LAST:
                    wo_chunks(st, (6, lambda: variance_of(5, U_ALL)))
                    return
                turn_v(st)
                wo_chunks(st, None if job is None else (0, lambda: variance_of(job, st.unit(0) + 4)))

            def tile_steps(tile):
                with pe.Fori(0, 3) as it:
                    for q in range(2):
                        step(Step(tile, it, q))
                step(Step(tile, 3, 0), job=tile + 1)

            pe.wait_ge(in_const, 16 * 5)
            first_norm()
            for j in range(6):
                project(First(), FIRST_ORDER[j], j, x_count=0 if j == 0 else None)
            turn_v(First())
            with pe.Fori(0, TT - 1) as tile:
                tile_steps(tile)
                step(Step(tile, 3, 1), x_job=tile + 1)
            tile_steps(TT - 1)
            step(LAST, x_job=4)
            for c in range(6, TT * A8):
                t_, o = c // A8, c % A8
                midway = None
                for n in (6, 7):
                    if c == mean_at(n):
                        midway = lambda n=n: mean_of(n, U_ALL)
                    if c == mean_at(n) + 3:
                        variance_of(n, U_ALL)
                project(LAST, *ffn_chunk(c), x=x_of(4 + t_), x_count=8 * (4 + t_) if o == 0 else None,
                        midway=midway)

        @block.scalar
        def _(act):
            def copy(dst, src, done):
                nc.scalar.activation(dst, src, ACT.Copy).then_inc(done, 1)

            def weights(st, j):
                if not (isinstance(st, First) and j < NSPLIT):
                    act.wait_ge(chunk_ready, st.slot_free(j))
                act.wait_ge(raw_in[j % NRAW], st.raw_uses(j) * 16)
                copy(wh[:, st.split_slot(j), :], raw[:, j % NRAW, :], w_hi)

            def squares(n, src, read, some=range(A8)):
                for a in some:
                    act.wait_ge(dev_ready, n * 8 + (a + 1))
                    if a >= 2:
                        act.wait_ge(read, n * 8 + (a - 1) if read is var_step else n * 8 + (a - 9))
                    nc.scalar.activation(sq[:, a % 2, :], src[:, a, :], ACT.Square).then_inc(sq_ready, 1)

            def read_mean(n):
                act.wait_ge(mean_ready, n + 1)
                copy(mean[:], mean_ps, mean_read)

            def deviation(n):
                act.wait_ge(rstd_step, n * 2 + 1)
                nc.scalar.activation(rstd[:], rstd[:], ACT.Sqrt).then_inc(std_ready, 1)

            def x_high(n, dst, src, some):
                for a in some:
                    if isinstance(n, int) and n == 0:
                        if a % 2:
                            act.wait_ge(first_odd, a // 2 + 1)
                        else:
                            act.wait_ge(norm_ready, a + 2)
                    else:
                        act.wait_ge(norm_ready, n * 8 + (a + 1))
                    copy(dst[0][:, a, :], src[:, a, :], x_hi)

            def rotate(st, j, m):
                act.wait_ge(chunk_ready, st.chunk(j) + 1)
                ps = chunk_ps[st.bank(j)]
                nc.scalar.activation(rot[0:64, :], ps[64:128, :], ACT.Copy)
                nc.scalar.activation(rot[64:128, :], ps[0:64, :], ACT.Copy).then_inc(rot_ready, 1)

            def rope_hi(st, j, m):
                act.wait_ge(rope_ready, st.heads() * 5 + (m + 1))
                dst = kh[:, st.new, :] if j == 0 else qh[:, st.new, j - 2, :]
                copy(dst, roped[:], r_hi)

            def v_split(st):
                act.wait_ge(turn_ready, st.heads() * 5 + 1)
                copy(vh[:, st.new, :], turn_ps[:], v_hi)

            def exps(st, u):
                act.wait_ge(max_ready, st.unit(u) + 1)
                for h in range(GQ):
                    x = prob[:, u % 2, h, :]
                    last = nc.scalar.activation(x, x, ACT.Exp, bias=stat[:, u % 2, 0, h:h + 1], scale=QSCALE,
                                                accum_out=stat[:, u % 2, 1, h:h + 1])
                last.then_inc(exp_ready, 1)

            def probs_hi(st, u):
                act.wait_ge(turn_ready, st.heads() * 5 + (u - 3))
                copy(pth[:], turn_ps[:], pt_hi)

            def attn_hi(st, u):
                act.wait_ge(attn_ready, st.unit(u) + 1)
                if u == 0:
                    act.wait_ge(chunk_ready, st.chunk(0))
                copy(oh[:, :, u * SEQ:(u + 1) * SEQ], attn_ps[:].rearrange("p (h s) -> p h s", h=GQ), o_hi)

            def step(st, job=None):
                ffn = st is LAST

                def some_squares(i):
                    if job is not None:
                        squares(job, dev, sq_read, range(2 * i, 2 * i + 2))

                weights(st, 3)
                exps(st, 0)
                if job is not None:
                    read_mean(job)
                if not ffn:
                    rotate(st, 0, 0)
                exps(st, 1)
                probs_hi(st, 0)
                weights(st, 4)
                if not ffn:
                    rope_hi(st, 0, 0)
                attn_hi(st, 0)
                probs_hi(st, 1)
                exps(st, 2)
                weights(st, 5)
                some_squares(0)
                if not ffn:
                    rotate(st, 2, 1)
                attn_hi(st, 1)
                probs_hi(st, 2)
                exps(st, 3)
                weights(st, 6)
                some_squares(1)
                if not ffn:
                    rope_hi(st, 2, 1)
                    rotate(st, 3, 2)
                attn_hi(st, 2)
                weights(st, 7)
                probs_hi(st, 3)
                some_squares(2)
                if ffn:
                    read_mean(5)
                else:
                    rope_hi(st, 3, 2)
                    rotate(st, 4, 3)
                weights(st, 8)
                attn_hi(st, 3)
                some_squares(3)
                if not ffn:
                    rope_hi(st, 4, 3)
                    rotate(st, 5, 4)
                    v_split(st)
                weights(st, 9)
                if ffn:
                    squares(5, dev, sq_read, range(0, 2))
                else:
                    rope_hi(st, 5, 4)
                if job is not None:
                    deviation(job)
                weights(st, 10)
                if ffn:
                    squares(5, dev, sq_read, range(2, 5))
                if job is not None:
                    x_high(job, (xh, xl), dev, range(0, 4))
                weights(st, 11)
                if ffn:
                    squares(5, dev, sq_read, range(5, 8))
                if job is not None:
                    x_high(job, (xh, xl), dev, range(4, 8))
                weights(st, 12)
                if ffn:
                    deviation(5)

            def tile_steps(tile):
                with act.Fori(0, 3) as it:
                    for q in range(2):
                        step(Step(tile, it, q))
                step(Step(tile, 3, 0), tile + 1)

            first, second = First(), Step(0, 0, 0)
            for j in range(NRAW):
                weights(first, j)
            squares(0, dev, var_step)
            deviation(0)
            x_high(0, (xh, xl), dev, range(A8))
            weights(first, NRAW)
            act.wait_ge(h_stored, 16 * H_STORES)
            for j in range(6):
                weights(*((first, j + 3) if j < 3 else (second, j - 3)))
                if j >= 1:
                    rotate(first, FIRST_ORDER[j - 1], j - 1)
                    rope_hi(first, FIRST_ORDER[j - 1], j - 1)
            v_split(first)
            with act.Fori(0, TT - 1) as tile:
                tile_steps(tile)
                step(Step(tile, 3, 1))
            tile_steps(TT - 1)
            step(LAST)
            for c in range(6, TT * A8):
                t_, o = c // A8, c % A8
                if c in (6, 7):
                    x_high(5, x_of(5), dev, range(4 * (c - 6), 4 * (c - 5)))
                for n, src in ((6, acc), (7, dev)):
                    stage = c - mean_at(n)
                    if stage == 0:
                        read_mean(n)
                    if stage in (1, 2):
                        squares(n, src, sq_read, range(4 * (stage - 1), 4 * stage))
                    if stage == 3:
                        deviation(n)
                    if stage == 4:
                        x_high(n, x_of(n), src, range(A8))
                if c + 7 < 10 + TT * A8 - 6:
                    weights(LAST, c + 7)

        @block.vector
        def _(dve):
            v = nc.vector

            def split_lo(dst, src, hi, done):
                v.tensor_tensor(dst, src, hi.bitcast(F32), ALU.subtract).then_inc(done, 1)

            def weights(st, j):
                slot = st.split_slot(j)
                dve.wait_ge(w_hi, st.tile(j) + 1)
                split_lo(wl[:, slot, :], raw[:, j % NRAW, :], wh[:, slot, :], w_lo)

            def deviation(n):
                if isinstance(n, int) and n == 0:
                    dve.wait_ge(var_step, A8)
                else:
                    dve.wait_ge(var_ready, n)
                v.tensor_scalar(rstd[:], var_ps, EPS, None, ALU.add).then_inc(rstd_step, 1)

            def invert(n):
                dve.wait_ge(std_ready, n + 1)
                v.reciprocal(rstd[:], rstd[:]).then_inc(rstd_step, 1)

            def x_low(n, dst, src, some):
                for a in some:
                    dve.wait_ge(x_hi, n * 8 + (a + 1))
                    split_lo(dst[1][:, a, :], src[:, a, :], dst[0][:, a, :], x_lo)

            def first_norm():
                dve.wait_ge(mean_ready, 1)
                for a in range(A8):
                    v.tensor_tensor(dev[:, a, :], acc[:, a, :], mean_ps, ALU.subtract).then_inc(dev_ready, 1)
                deviation(0)
                invert(0)
                dve.wait_ge(rstd_step, 2)
                for a in range(0, A8, 2):
                    v.tensor_tensor(dev[:, a, :], dev[:, a, :], rstd[:], ALU.mult).then_inc(norm_ready, 2)
                    if a >= 2:
                        x_low(0, (xh, xl), dev, [a - 2, a - 1])
                x_low(0, (xh, xl), dev, [A8 - 2, A8 - 1])

            def rope(st, j, m):
                def seqs(x):
                    return x.rearrange("p (c s) -> p c s", c=CPT)

                def table(x):
                    return x[:].unsqueeze(1).broadcast_to([P, CPT, SEQ])

                ps = chunk_ps[st.bank(j)]
                dve.wait_ge(rot_ready, st.heads() * 5 + (m + 1))
                v.tensor_tensor(seqs(direct[:]), seqs(ps[:]), table(cos), ALU.mult).then_inc(chunk_free, 1)
                v.tensor_tensor(seqs(rot[:]), seqs(rot[:]), table(sin), ALU.mult).then_inc(rope_step, 1)
                dve.wait_ge(rope_step, st.heads() * 5 + (m + 1))
                v.tensor_tensor(roped[:], direct[:], rot[:], ALU.add).then_inc(rope_ready, 1)

            def rope_lo(st, j, m):
                dve.wait_ge(r_hi, st.heads() * 5 + (m + 1))
                hi, lo = (x[:, st.new, :] if j == 0 else y[:, st.new, j - 2, :] for x, y in ((kh, qh), (kl, ql)))
                split_lo(lo, roped[:], hi, r_lo)

            def v_copy(st):
                dve.wait_ge(chunk_ready, st.chunk(1) + 1)
                v.tensor_copy(vt[:], chunk_ps[st.bank(1)][:]).then_inc(chunk_free, 1)

            def v_split(st):
                dve.wait_ge(v_hi, st.heads() + 1)
                split_lo(vl[:, st.new, :], turn_ps[:], vh[:, st.new, :], turn_free)

            def maxima(st, u):
                dve.wait_ge(score_ready, st.unit(u) + 1)
                causal = mask[:].unsqueeze(1).broadcast_to([P, GQ, SEQ])
                v.tensor_tensor(prob[:, u % 2], score_of[:, :, 1], causal, ALU.add).then_inc(mask_step, 1)
                dve.wait_ge(mask_step, st.unit(u) + 1)
                v.tensor_tensor(prob[:, u % 2], score_of[:, :, 0], prob[:, u % 2], ALU.add).then_inc(score_free, 1)
                dve.wait_ge(score_free, st.unit(u) + 2)
                v.reduce_max(stat[:, u % 2, 0, :], prob[:, u % 2], mybir.AxisListType.X).then_inc(max_step, 1)
                dve.wait_ge(max_step, st.unit(u) + 1)
                v.tensor_scalar(stat[:, u % 2, 0, :], stat[:, u % 2, 0, :], -QSCALE, None,
                                ALU.mult).then_inc(max_ready, 1)

            def normalise(st, u):
                dve.wait_ge(exp_ready, st.unit(u) + 1)
                v.reciprocal(stat[:, u % 2, 2, :], stat[:, u % 2, 1, :]).then_inc(inv_step, 1)
                dve.wait_ge(inv_step, st.unit(u) + 1)
                v.tensor_tensor(prob[:, u % 2], prob[:, u % 2],
                                stat[:, u % 2, 2, :].unsqueeze(2).broadcast_to([P, GQ, SEQ]),
                                ALU.mult).then_inc(prob_ready, 1)

            def probs_lo(st, u):
                dve.wait_ge(pt_hi, st.unit(u) + 1)
                split_lo(ptl[:], turn_ps[:], pth[:], turn_free)

            def attn_lo(st, u):
                dve.wait_ge(o_hi, st.unit(u) + 1)
                tok = slice(u * SEQ, (u + 1) * SEQ)
                split_lo(ol[:, :, tok], attn_ps[:].rearrange("p (h s) -> p h s", h=GQ), oh[:, :, tok], attn_free)

            def add_chunk(st, o):
                if o == 0:
                    dve.wait_ge(acc_tiles, st.tile_no * 1 + 1)
                dve.wait_ge(chunk_ready, st.chunk(6 + o) + 1)
                v.tensor_tensor(acc[:, o, :], acc[:, o, :], chunk_ps[st.bank(6 + o)][:], ALU.add).then_inc(chunk_free, 1)

            def result(c):
                m, slot = ffn_chunk(c)[0], c % NRES
                dve.wait_ge(res_in[slot], 16 * (c // NRES + 1))
                dve.wait_ge(chunk_ready, LAST.chunk(m) + 1)
                v.scalar_tensor_tensor(res[:, slot, :], chunk_ps[LAST.bank(m)][:], bias[:, c % A8:c % A8 + 1],
                                       res[:, slot, :], ALU.add, ALU.add).then_inc(chunk_free, 1)

            def step(st, job=None):
                ffn = st is LAST
                maxima(st, 0)
                weights(st, 3)
                normalise(st, 0)
                maxima(st, 1)
                if ffn:
                    result(0)
                else:
                    rope(st, 0, 0)
                probs_lo(st, 0)
                normalise(st, 1)
                weights(st, 4)
                if not ffn:
                    rope_lo(st, 0, 0)
                maxima(st, 2)
                attn_lo(st, 0)
                probs_lo(st, 1)
                if ffn:
                    result(1)
                else:
                    v_copy(st)
                normalise(st, 2)
                weights(st, 5)
                maxima(st, 3)
                attn_lo(st, 1)
                probs_lo(st, 2)
                if ffn:
                    result(2)
                else:
                    rope(st, 2, 1)
                normalise(st, 3)
                weights(st, 6)
                if ffn:
                    result(3)
                else:
                    rope_lo(st, 2, 1)
                    rope(st, 3, 2)
                attn_lo(st, 2)
                weights(st, 7)
                probs_lo(st, 3)
                if ffn:
                    result(4)
                else:
                    rope_lo(st, 3, 2)
                    rope(st, 4, 3)
                weights(st, 8)
                attn_lo(st, 3)
                if not ffn:
                    rope_lo(st, 4, 3)
                    rope(st, 5, 4)
                    v_split(st)
                weights(st, 9)
                if ffn:
                    result(5)
                else:
                    rope_lo(st, 5, 4)
                for o in range(A8):
                    add_chunk(st, o)
                    if o == 1:
                        if job is not None:
                            deviation(job)
                            invert(job)
                        weights(st, 10)
                    if o == 3:
                        if job is not None:
                            x_low(job, (xh, xl), dev, range(0, 4))
                        weights(st, 11)
                    if o == 5:
                        if job is not None:
                            x_low(job, (xh, xl), dev, range(4, 8))
                        weights(st, 12)
                    if ffn and o == 6:
                        deviation(5)
                        invert(5)

            def tile_steps(tile):
                with dve.Fori(0, 3) as it:
                    for q in range(2):
                        step(Step(tile, it, q))
                step(Step(tile, 3, 0), tile + 1)

            for given, count in ((w_lo, NRAW), (chunk_free, NCHUNK), (turn_free, 1), (score_free, 1), (attn_free, 1),
                                 (acc_tiles, 1)):
                dve.sem_inc(given, count)
            dve.wait_ge(in_const, 16 * 5)
            first, second = First(), Step(0, 0, 0)
            for a in range(A8 // 2 + 1, A8):
                if a > A8 // 2 + 1:
                    dve.wait_ge(first_sum, a - A8 // 2 - 1)
                v.tensor_tensor(total[:], acc[:, a - 1, :] if a == A8 // 2 + 1 else total[:], acc[:, a, :],
                                ALU.add).then_inc(first_sum, 1)
            for j in range(NRAW):
                weights(first, j)
            first_norm()
            weights(first, NRAW)
            for j in range(6):
                weights(*((first, j + 3) if j < 3 else (second, j - 3)))
                if j >= 1:
                    rope(first, FIRST_ORDER[j - 1], j - 1)
                    rope_lo(first, FIRST_ORDER[j - 1], j - 1)
            v_copy(first)
            v_split(first)
            with dve.Fori(0, TT - 1) as tile:
                tile_steps(tile)
                step(Step(tile, 3, 1))
            tile_steps(TT - 1)
            step(LAST)
            for c in range(6, TT * A8):
                t_, o = c // A8, c % A8
                if c in (6, 7):
                    x_low(5, x_of(5), dev, range(4 * (c - 6), 4 * (c - 5)))
                for n, src in ((6, acc), (7, dev)):
                    stage = c - mean_at(n)
                    if stage == -1:
                        sums(v, dve, n, src)
                    if stage in (1, 2):
                        square_sums(v, dve, n, range(1, 4) if stage == 1 else range(4, 8))
                    if stage == 3:
                        deviation(n)
                        invert(n)
                    if stage == 4:
                        x_low(n, x_of(n), src, range(A8))
                if c + 7 < 10 + TT * A8 - 6:
                    weights(LAST, c + 7)
                result(c)


class Kept:

    def __init__(self, nc, ctx):
        def sb(name, shape):
            return ctx.enter_context(nc.sbuf_tensor(name, shape, F32))

        def sem(name):
            return ctx.enter_context(nc.semaphore(name))

        self.acc = sb("acc", [P, A8, NT])
        self.raw = sb("raw", [P, NRAW, D])
        self.cos, self.sin = sb("cos", [P, SEQ]), sb("sin", [P, SEQ])
        self.mask, self.ident = sb("mask", [P, SEQ]), sb("ident", [P, P])
        self.mean_w = sb("mean_w", [P, P])
        self.bias = sb("bias", [P, A8])
        self.h_stored, self.in_const = sem("h_stored"), sem("in_const")
        self.raw_in = [sem(f"raw_in{i}") for i in range(NRAW)]


def program(nc, ins, out_dram, h_dram, weff_dram):
    with ExitStack() as ctx:
        kept = Kept(nc, ctx)
        s4d_and_lora_fold(nc, ins, kept, h_dram, weff_dram)
        transformer(nc, ins, kept, h_dram, weff_dram, out_dram)


def constants():
    f = np.float32
    tab = np.concatenate([np.arange(B0), B0 * np.arange(B1), P * np.arange(A8)]).astype(f)
    inv_freq = f(1.0) / f(10000.0) ** (np.arange(0, HD, 2, dtype=f) / f(HD))
    freqs = np.arange(SEQ, dtype=f)[:, None] * inv_freq[None, :]
    emb = np.concatenate([freqs, freqs], axis=-1)
    cos, sin = np.cos(emb).astype(f).T, np.sin(emb).astype(f).T
    sign = np.where(np.arange(HD) < HD // 2, f(-1), f(1))[:, None]
    pos = np.arange(SEQ)
    return {
        "tab": np.broadcast_to(tab, (P, NTAB)).copy(),
        "cos": cos.copy(), "sin": (sin * sign).astype(f),
        "mask": np.where(pos[:, None] >= pos[None, :], f(0), np.finfo(f).min).astype(f),
        "ident": np.eye(P, dtype=f),
        "mean_w": np.full((P, P), 1.0 / D, f),
    }


def kernel(x, L0_tok_log_dt, L0_tok_B, L0_tok_inv_A_real, L0_tok_A_imag, L0_attn_wq, L0_attn_wk, L0_attn_wv,
           L0_attn_wo, L0_ffn_W, L0_ffn_bias, L0_ffn_A, L0_ffn_Bf, L0_ffn_coeffs, L0_ffn_scales):
    import concourse.bacc as bacc
    from concourse.bass_utils import run_bass_kernel_spmd

    def both(y):
        return np.concatenate([np.asarray(y).T] * 2, axis=0)

    c = np.asarray(x).transpose(3, 2, 1, 0)
    b = np.asarray(L0_tok_B)
    wq = np.asarray(L0_attn_wq).reshape(NKV, GQ, HD, A8, P)
    wk = np.asarray(L0_attn_wk).reshape(NKV, 1, HD, A8, P)
    wv = np.asarray(L0_attn_wv).reshape(NKV, 1, HD, A8, P)
    wqkv = np.concatenate([wk, wv, wq], axis=1).transpose(0, 1, 4, 3, 2).reshape(NKV, 6, P, D)
    wo = np.asarray(L0_attn_wo).reshape(4, 256, NKV, GQ, HD).transpose(2, 0, 4, 3, 1).reshape(NKV, 4, P, D)
    per_expert = [np.repeat(np.asarray(y), ER // 16).reshape(2, P).T for y in (L0_ffn_coeffs, L0_ffn_scales)]
    arrays = {
        "small": np.stack([np.broadcast_to(np.asarray(L0_tok_log_dt), (P, SEQ)), both(L0_tok_inv_A_real),
                           both(L0_tok_A_imag), both(b[..., 0]), both(b[..., 1])], axis=1),
        "coef": np.concatenate([c.transpose(1, 0, 2, 3)] * 2, axis=0),
        "lora_a": np.asarray(L0_ffn_A).reshape(2, P, D).transpose(1, 0, 2),
        "lora_b": np.asarray(L0_ffn_Bf).transpose(0, 2, 1).reshape(2, P, D).transpose(1, 0, 2),
        "lora_w": np.concatenate(per_expert, axis=1),
        "wt": np.asarray(L0_ffn_W).T.reshape(A8, P, D),
        "wqkv": wqkv, "wo": wo,
        "bias": np.asarray(L0_ffn_bias).reshape(A8, P).T,
    }
    arrays.update(constants())
    arrays = {k: np.ascontiguousarray(v) for k, v in arrays.items()}

    nc = bacc.Bacc("TRN2", target_bir_lowering=False, num_devices=1)
    ins = {k: nc.dram_tensor(f"in_{k}", v.shape, mybir.dt.from_np(v.dtype), kind="ExternalInput").ap()
           for k, v in arrays.items()}
    out = nc.dram_tensor("out_t", (TT, A8, P, NT), F32, kind="ExternalOutput").ap()
    h_dram = nc.dram_tensor("h_t", (TT, P, A8, NT), F32, kind="Internal").ap()
    weff = nc.dram_tensor("weff", (A8, P, A8, P), F32, kind="Internal").ap()
    program(nc, ins, out, h_dram, weff)
    r = run_bass_kernel_spmd(nc, [{f"in_{k}": v for k, v in arrays.items()}], core_ids=[0])
    y = r.results[0]["out_t"].reshape(TT, D, CPT, SEQ)
    return y.transpose(0, 2, 3, 1).reshape(NB, SEQ, D)
```
